# Optimizing a Trainium2 kernel written in Bass

```python
import numpy as np
import jax
import jax.numpy as jnp

def _softmax(x, axis=-1):
    return jax.nn.softmax(x, axis=axis)

def _gelu(x):
    return jax.nn.gelu(x, approximate=True)

def _silu(x):
    return jax.nn.silu(x)

def _sigmoid(x):
    return jax.nn.sigmoid(x)

def _layernorm(x, axis=-1, eps=1e-05):
    m = jnp.mean(x, axis=axis, keepdims=True)
    v = jnp.var(x, axis=axis, keepdims=True)
    return (x - m) / jnp.sqrt(v + eps)

def _scatter_add(tgt, idx, src, axis=0):
    return tgt.at[idx].add(src)

def _segment_sum(src, seg, n):
    return jax.ops.segment_sum(src, seg, n)
kernel_name = 'mk_gnn_preln_d1_gnn_r64_c17fb7'

def setup_inputs(seed: int=0):
    np.random.seed(seed)
    _w = jnp.asarray

    def _rec_inputs():
        import jax
        import jax.numpy as jnp
        _gk = jax.random.key(seed)
        x = -0.0003929 + 0.9999 * jax.random.normal(jax.random.fold_in(_gk, 1), (256, 1024), jnp.float32)
        _s = jax.random.randint(jax.random.fold_in(_gk, 2), (4096,), 0, 256, jnp.int32)
        _d = jax.random.randint(jax.random.fold_in(_gk, 3), (4096,), 0, 256, jnp.int32)
        _loop = jnp.arange(256, dtype=jnp.int32)
        src = jnp.concatenate([_s, _d, _loop])
        dst = jnp.concatenate([_d, _s, _loop])
        _o = jnp.argsort(dst, stable=True)
        src = src[_o]
        dst = dst[_o]
        return (x, src, dst)
    x, src, dst = _rec_inputs()

    def _L0_gnn_setup():
        import jax, jax.numpy as jnp
        import numpy as np
        NH, NO = (64, 192)
        N = NH + NO
        E_HH, E_OO, E_HO = (128, 640, 256)
        E = E_HH + E_OO + E_HO
        D = 1024
        key = jax.random.key(seed)
        ks = jax.random.split(key, 12)
        w = lambda k, s: jax.random.normal(k, s, jnp.float32) * 0.02
        return {'n_f': jax.random.normal(ks[0], (N, D), jnp.float32), 'W_hh': w(ks[1], (2 * D, D)), 'b_hh': jnp.zeros((D,), jnp.float32), 'W_oo': w(ks[2], (2 * D, D)), 'b_oo': jnp.zeros((D,), jnp.float32), 'W_ho': w(ks[3], (2 * D, D)), 'b_ho': jnp.zeros((D,), jnp.float32), 'W_a': w(ks[4], (D, 1)), 'b_a': jnp.zeros((1,), jnp.float32), 'W_hn': w(ks[5], (2 * D, D)), 'b_hn': jnp.zeros((D,), jnp.float32), 'W_on': w(ks[6], (2 * D, D)), 'b_on': jnp.zeros((D,), jnp.float32), 'edge_src': jax.random.randint(ks[7], (E,), 0, N, jnp.int32), 'edge_dst': jax.random.randint(ks[8], (E,), 0, N, jnp.int32)}
    _L0_gnn_all = _L0_gnn_setup()
    _L0_gnn_in = {k: v for k, v in _L0_gnn_all.items() if k in ('W_hh', 'b_hh', 'W_oo', 'b_oo', 'W_ho', 'b_ho', 'W_a', 'b_a', 'W_hn', 'b_hn', 'W_on', 'b_on')}
    del _L0_gnn_all
    return {'x': x, 'src': src, 'dst': dst, 'L0_gnn_W_hh': _L0_gnn_in['W_hh'], 'L0_gnn_b_hh': _L0_gnn_in['b_hh'], 'L0_gnn_W_oo': _L0_gnn_in['W_oo'], 'L0_gnn_b_oo': _L0_gnn_in['b_oo'], 'L0_gnn_W_ho': _L0_gnn_in['W_ho'], 'L0_gnn_b_ho': _L0_gnn_in['b_ho'], 'L0_gnn_W_a': _L0_gnn_in['W_a'], 'L0_gnn_b_a': _L0_gnn_in['b_a'], 'L0_gnn_W_hn': _L0_gnn_in['W_hn'], 'L0_gnn_b_hn': _L0_gnn_in['b_hn'], 'L0_gnn_W_on': _L0_gnn_in['W_on'], 'L0_gnn_b_on': _L0_gnn_in['b_on']}

def reference(x, src, dst, L0_gnn_W_hh, L0_gnn_b_hh, L0_gnn_W_oo, L0_gnn_b_oo, L0_gnn_W_ho, L0_gnn_b_ho, L0_gnn_W_a, L0_gnn_b_a, L0_gnn_W_hn, L0_gnn_b_hn, L0_gnn_W_on, L0_gnn_b_on):
    import jax
    import jax.numpy as jnp

    def _L0_gnn_ref(n_f, W_hh, b_hh, W_oo, b_oo, W_ho, b_ho, W_a, b_a, W_hn, b_hn, W_on, b_on, edge_src, edge_dst):
        import jax, jax.numpy as jnp
        import numpy as np
        NH, NO = (64, 192)
        N = NH + NO
        E_HH, E_OO, E_HO = (128, 640, 256)
        E = E_HH + E_OO + E_HO
        D = 1024
        feat = jnp.concatenate([n_f[edge_src], n_f[edge_dst]], axis=1)
        e_hh = jax.nn.relu(feat[:E_HH] @ W_hh + b_hh)
        e_oo = jax.nn.relu(feat[E_HH:E_HH + E_OO] @ W_oo + b_oo)
        e_ho = jax.nn.relu(feat[E_HH + E_OO:] @ W_ho + b_ho)
        e_f = jnp.concatenate([e_hh, e_oo, e_ho], axis=0)
        logit = (e_f @ W_a + b_a)[:, 0]
        m = jax.lax.stop_gradient(jax.ops.segment_max(logit, edge_dst, num_segments=N))
        ex = jnp.exp(logit - m[edge_dst])
        den = jax.ops.segment_sum(ex, edge_dst, num_segments=N)
        alpha = ex / den[edge_dst]
        z_f = jax.ops.segment_sum(alpha[:, None] * n_f[edge_src], edge_dst, num_segments=N)
        nf2 = jnp.concatenate([n_f, z_f], axis=1)
        h_new = jax.nn.relu(nf2[:NH] @ W_hn + b_hn)
        o_new = jax.nn.relu(nf2[NH:] @ W_on + b_on)
        return jnp.concatenate([h_new, o_new], axis=0)
    h = jnp.maximum(_layernorm(x, axis=-1), 0.0)
    x = x + _L0_gnn_ref(h, L0_gnn_W_hh, L0_gnn_b_hh, L0_gnn_W_oo, L0_gnn_b_oo, L0_gnn_W_ho, L0_gnn_b_ho, L0_gnn_W_a, L0_gnn_b_a, L0_gnn_W_hn, L0_gnn_b_hn, L0_gnn_W_on, L0_gnn_b_on, src, dst)
    return x

_drawn_inputs = setup_inputs


def setup_inputs(seed=0):
    import zlib

    import numpy as np

    out = dict(_drawn_inputs(seed))
    spreads = {'L0_gnn_b_hh': (0.0, 2.0),
     'L0_gnn_b_oo': (0.0, 2.0),
     'L0_gnn_b_ho': (0.0, 0.8),
     'L0_gnn_b_hn': (0.0, 0.1),
     'L0_gnn_b_on': (0.0, 0.1)}
    factors = {'L0_gnn_W_hh': 21.779, 'L0_gnn_W_oo': 8.0, 'L0_gnn_W_ho': 8.0, 'L0_gnn_W_a': 8.0}
    for name, (base, spread) in spreads.items():
        noise = np.random.default_rng([zlib.crc32(name.encode()), seed]).standard_normal(out[name].shape)
        drawn = base * np.exp(spread * noise) if base else spread * noise
        out[name] = jnp.asarray(drawn.astype(out[name].dtype))
    for name, factor in factors.items():
        out[name] = (out[name] * factor).astype(out[name].dtype)
    return out
```

```python
from contextlib import ExitStack

import concourse.bass as bass
from concourse import mybir

ALU = mybir.AluOpType
ACT = mybir.ActivationFunctionType
AX = mybir.AxisListType
F32 = mybir.dt.float32
F32R = mybir.dt.float32r
I32 = mybir.dt.int32

P = 128
BANK = 512
EPS = 1e-5
ABSENT = -3.0e38
UNROLL = 4
RAW = 8
SPLIT = 2


def gnn_kernel(nc, x, src, dst, w_edge, b_edge, w_a, b_a, w_node, b_node, out, e_types, n_first):
    N, D = x.shape
    E = src.shape[0]
    NT = N // P
    KC = D // P
    ET = E // P
    HALVES = D // BANK
    first_tile = [sum(e_types[:i]) // P for i in range(len(e_types))]
    tiles_of = [e // P for e in e_types]
    NTYPE = len(e_types)
    assert N == 2 * P and D == 2 * BANK and all(e % P == 0 for e in e_types)

    ctx = ExitStack()
    with ctx:
        def sb(name, shape, dt=F32):
            return ctx.enter_context(nc.sbuf_tensor(name, shape, dt))

        def sem(name):
            return ctx.enter_context(nc.semaphore(name))

        x_sb = sb("x_sb", [P, NT, D])
        h_sb = sb("h_sb", [P, NT, D])
        nfT_hi = sb("nfT_hi", [P, 2 * KC, N], F32R)
        nfT_lo = sb("nfT_lo", [P, 2 * KC, N], F32R)
        w_raw = sb("w_raw", [P, RAW, D])
        w_hi = sb("w_hi", [P, SPLIT, D], F32R)
        w_lo = sb("w_lo", [P, SPLIT, D], F32R)
        table = sb("table", [P, 2, NT, 2, D], F32R)
        biased = sb("biased", [P, NT, D])
        bias = sb("bias", [P, 2, D])
        wa_row = sb("wa_row", [P, D])
        ba_col = sb("ba_col", [P, 1])
        junk = biased[:, 0, :]
        ids_rows_i = sb("ids_rows_i", [ET, 2, P], I32)
        ids_rows = sb("ids_rows", [ET, 2, P])
        ids = sb("ids", [P, 2, ET])
        iota_i = sb("iota_i", [P, N], I32)
        iota_row = sb("iota_row", [P, N])
        ident = sb("ident", [P, P])
        ident_r = sb("ident_r", [P, P], F32R)
        zeros_r = sb("zeros_r", [P, N], F32R)
        hot = sb("hot", [P, UNROLL, 4, N], F32R)
        hotT = sb("hotT", [P, 2, 4, P], F32R)
        logit = sb("logit", [P, UNROLL])
        stats = sb("stats", [P, 10, NT])
        pairs = sb("pairs", [P, NT, NTYPE, 2, N])
        shifted = sb("shifted", [P, NT, NTYPE * N])
        soft = sb("soft", [P, 3, NTYPE * N])
        small = sb("small", [P, 8, NT])
        alpha = sb("alpha", [P, NT, N])
        alphaT = sb("alphaT", [P, NT, N])
        out_sb = h_sb

        psum = ctx.enter_context(nc.psum_tensor("psum", [P, 8, BANK], F32))
        pz = [psum[:, 2 * b:2 * b + 2, :].rearrange("p a n -> p (a n)") for b in range(2)]
        p_pair = [psum[:, 4 + c, :] for c in range(NT)]
        p_tr = [psum[:, 6 + b, :] for b in range(2)]

        x_in = sem("x_in")
        ids_in = sem("ids_in")
        small_in = sem("small_in")
        bias_in = sem("bias_in")
        w_in = [sem(f"w_in{i}") for i in range(RAW)]
        consts = sem("consts")
        dve_step = sem("dve_step")
        act_step = sem("act_step")
        pool_step = sem("pool_step")
        ids_f = sem("ids_f")
        ids_T = sem("ids_T")
        ids_ready = sem("ids_ready")
        sum_ready = sem("sum_ready")
        sq_ready = sem("sq_ready")
        var_ready = sem("var_ready")
        std_ready = sem("std_ready")
        norm_ready = sem("norm_ready")
        h_ready = sem("h_ready")
        hT_done = sem("hT_done")
        hT_hi = sem("hT_hi")
        hT_lo = sem("hT_lo")
        hi_ready = sem("hi_ready")
        lo_ready = sem("lo_ready")
        chunk_used = sem("chunk_used")
        prod_done = sem("prod_done")
        tb_biased = sem("tb_biased")
        tb_hi = sem("tb_hi")
        tb_lo = sem("tb_lo")
        hot_ready = sem("hot_ready")
        tr_done = sem("tr_done")
        hotT_ready = sem("hotT_ready")
        gather_done = sem("gather_done")
        logit_ready = sem("logit_ready")
        shi_ready = sem("shi_ready")
        scaled_ready = sem("scaled_ready")
        scatter_done = sem("scatter_done")
        pairs_open = sem("pairs_open")
        pairs_ready = sem("pairs_ready")
        exp_bias = sem("exp_bias")
        exp_done = sem("exp_done")
        alpha_ready = sem("alpha_ready")
        alphaT_done = sem("alphaT_done")
        alphaT_ready = sem("alphaT_ready")
        z_done = sem("z_done")
        z_hi = sem("z_hi")
        z_lo = sem("z_lo")
        y_done = sem("y_done")
        y_biased = sem("y_biased")
        out_ready = sem("out_ready")
        out_saved = sem("out_saved")

        weights = list(w_edge) + list(w_node)
        CH = 2 * KC

        def row(v):
            return v.rearrange("(a d) -> a d", a=1).broadcast_to([P, v.shape[0]])

        def tiles(eng, first, count, step):
            rounds = count // UNROLL
            if rounds >= 2:
                with eng.Fori(0, rounds) as r:
                    for j in range(UNROLL):
                        step(r * UNROLL + (first + j), (first + j) % UNROLL)
            else:
                rounds = 0
            for t in range(first + rounds * UNROLL, first + count):
                step(t, t % UNROLL)

        block = ctx.enter_context(nc.Block())

        @block.sync
        def _(sp):
            sp.dma_start(x_sb[:, :, :], x.rearrange("(t p) d -> p t d", p=P)).then_inc(x_in, 16)

            def load(m, half, c, g):
                rows = weights[m][bass.ds(half * D + c * P, P), :]
                sp.dma_start(w_raw[:, c % RAW, :], rows).then_inc(w_in[c % RAW], 16)

            for m in range(len(weights)):
                def half_matrix(half, base):
                    for c in range(KC):
                        if not (isinstance(base, int) and base + c < RAW):
                            sp.wait_ge(lo_ready, base + (c + 1 - RAW))
                        load(m, half, c, None)
                if m == 0:
                    for half in range(2):
                        half_matrix(half, half * KC)
                else:
                    with sp.Fori(0, 2) as half:
                        half_matrix(half, half * KC + m * CH)
            sp.wait_ge(out_ready, 1)
            sp.dma_start(out[0:n_first, :], out_sb[0:n_first, 0, :]).then_inc(out_saved, 16)
            sp.wait_ge(out_ready, 3)
            sp.dma_start(out[n_first:P, :], out_sb[n_first:P, 0, :]).then_inc(out_saved, 16)
            sp.dma_start(out[P:N, :], out_sb[:, 1, :]).then_inc(out_saved, 16)
            sp.wait_ge(out_saved, 48)

        @block.gpsimd
        def _(pool):
            nc.gpsimd.dma_start(ids_rows_i[:, 0, :], src.rearrange("(t e) -> t e", e=P)).then_inc(ids_in, 16)
            nc.gpsimd.dma_start(ids_rows_i[:, 1, :], dst.rearrange("(t e) -> t e", e=P)).then_inc(ids_in, 16)
            nc.gpsimd.iota(iota_i[:, :], pattern=[[1, N]], base=0, channel_multiplier=0).then_inc(pool_step, 1)
            nc.gpsimd.memset(ident[:, :], 0.0).then_inc(pool_step, 1)
            nc.gpsimd.memset(zeros_r[:, :].bitcast(F32), 0.0).then_inc(consts, 1)
            pool.wait_ge(pool_step, 2)
            nc.gpsimd.affine_select(out=ident[:, :], in_=ident[:, :], compare_op=ALU.not_equal, fill=1.0, base=0,
                                    pattern=[[-1, P]], channel_multiplier=1).then_inc(consts, 1)
            nc.gpsimd.tensor_copy(iota_row[:, :], iota_i[:, :]).then_inc(consts, 1)
            pool.wait_ge(consts, 3)
            nc.gpsimd.tensor_copy(ident_r[:, :], ident[:, :]).then_inc(consts, 1)
            nc.gpsimd.dma_start(wa_row[:, :], row(w_a.rearrange("d a -> (d a)"))).then_inc(small_in, 16)
            nc.gpsimd.dma_start(ba_col[:, :], row(b_a)).then_inc(small_in, 16)
            nc.gpsimd.dma_start(bias[:, 1, :], row(b_node[0])).then_inc(small_in, 16)
            for m, b in enumerate(list(b_edge) + [b_node[1]]):
                if m:
                    pool.wait_ge(tb_biased, 2 * m)
                nc.gpsimd.dma_start(bias[:, 0, :], row(b)).then_inc(bias_in, 16)

        @block.scalar
        def _(act):
            for t in range(NT):
                act.wait_ge(sum_ready, 1)
                nc.scalar.activation(biased[:, t, :], x_sb[:, t, :], ACT.Square, bias=stats[:, 1, t:t + 1],
                                     accum_out=stats[:, 2, t:t + 1]).then_inc(sq_ready, 1)
            act.wait_ge(var_ready, 1)
            nc.scalar.activation(stats[:, 4, :], stats[:, 3, :], ACT.Sqrt).then_inc(std_ready, 1)
            act.wait_ge(norm_ready, 1)
            for t in range(NT):
                nc.scalar.activation(h_sb[:, t, :], x_sb[:, t, :], ACT.Relu, bias=stats[:, 9, t:t + 1],
                                     scale=stats[:, 8, t:t + 1]).then_inc(h_ready, 1)
            for k in range(0, KC, 2):
                act.wait_ge(hT_done, k // 2 + 1)
                nc.scalar.copy(nfT_hi[:, k:k + 2, :].rearrange("p k n -> p (k n)"),
                               psum[:, 4 + k // 2, :]).then_inc(hT_hi, 1)

            def high_parts(half_index, first):
                for c in range(KC):
                    act.wait_ge(w_in[c % RAW], half_index * 16 + 16)
                    if not (first and c < SPLIT):
                        act.wait_ge(chunk_used, half_index * KC + (c + 1 - SPLIT))
                    nc.scalar.copy(w_hi[:, c % SPLIT, :], w_raw[:, c % RAW, :]).then_inc(hi_ready, 1)

            def transposed(t, q):
                b = q % 2
                act.wait_ge(tr_done, t + 1)
                if not (isinstance(t, int) and t < 2):
                    act.wait_ge(gather_done, t - 1)
                nc.scalar.copy(hotT[:, b, :, :].rearrange("p c e -> p (c e)"), p_tr[b]).then_inc(hotT_ready, 1)

            for m in range(NTYPE):
                for end in range(2):
                    s = 2 * m + end
                    high_parts(s, s == 0)
                    act.wait_ge(tb_biased, s + 1)
                    for t in range(NT):
                        if s >= 2 and s % 2 == 0 and t == 0:
                            act.wait_ge(gather_done, first_tile[m])
                        nc.scalar.copy(table[:, end, t, 0, :], biased[:, t, :]).then_inc(tb_hi, 1)
                tiles(act, first_tile[m], tiles_of[m], transposed)
                act.wait_ge(scatter_done, first_tile[m] + tiles_of[m])
                for c in range(NT):
                    nc.scalar.copy(pairs[:, c, m, :, :].rearrange("p a n -> p (a n)"), p_pair[c]).then_inc(pairs_ready, 1)

            high_parts(2 * NTYPE, False)
            for c in range(NT):
                act.wait_ge(exp_bias, 1)
                nc.scalar.activation(shifted[:, c, :], shifted[:, c, :], ACT.Exp,
                                     bias=small[:, 1, c:c + 1]).then_inc(exp_done, 1)
            act.wait_ge(alphaT_done, 1)
            nc.scalar.copy(alphaT[:, :, :].rearrange("p c n -> p (c n)"), psum[:, 0, :]).then_inc(alphaT_ready, 1)
            for k in range(0, KC, 2):
                act.wait_ge(z_done, k // 2 + 1)
                nc.scalar.copy(nfT_hi[:, KC + k:KC + k + 2, :].rearrange("p k n -> p (k n)"),
                               psum[:, 4 + k // 2, :]).then_inc(z_hi, 1)
            for i in range(1, 4):
                high_parts(2 * NTYPE + i, False)

        @block.vector
        def _(dve):
            step = [0]

            def own(ins):
                step[0] += 1
                ins.then_inc(dve_step, 1)
                dve.wait_ge(dve_step, step[0])

            dve.wait_ge(ids_in, 32)
            nc.vector.tensor_copy(ids_rows[:, :, :], ids_rows_i[:, :, :]).then_inc(ids_f, 1)
            dve.wait_ge(x_in, 16)
            own(nc.vector.tensor_reduce(stats[:, 0, :], x_sb[:, :, :], AX.X, ALU.add))
            nc.vector.tensor_scalar(stats[:, 1, :], stats[:, 0, :], -1.0 / D, None, ALU.mult).then_inc(sum_ready, 1)
            dve.wait_ge(ids_T, 1)
            nc.vector.tensor_copy(ids[:, :, :], p_tr[0][:, 0:2 * ET].rearrange("p (a t) -> p a t", a=2)).then_inc(ids_ready, 1)
            dve.wait_ge(sq_ready, NT)
            nc.vector.tensor_scalar(stats[:, 3, :], stats[:, 2, :], 1.0 / D, EPS, ALU.mult, ALU.add).then_inc(var_ready, 1)
            dve.wait_ge(std_ready, 1)
            own(nc.vector.reciprocal(stats[:, 5, :], stats[:, 4, :]))
            own(nc.vector.tensor_tensor(stats[:, 6, :], stats[:, 5, :], stats[:, 5, :], ALU.mult))
            own(nc.vector.tensor_tensor(stats[:, 7, :], stats[:, 6, :], stats[:, 3, :], ALU.mult))
            own(nc.vector.tensor_scalar(stats[:, 6, :], stats[:, 7, :], -0.5, 1.5, ALU.mult, ALU.add))
            own(nc.vector.tensor_tensor(stats[:, 8, :], stats[:, 5, :], stats[:, 6, :], ALU.mult))
            nc.vector.tensor_tensor(stats[:, 9, :], stats[:, 8, :], stats[:, 1, :], ALU.mult).then_inc(norm_ready, 1)
            for k in range(0, KC, 2):
                dve.wait_ge(hT_hi, k // 2 + 1)
                nc.vector.tensor_tensor(nfT_lo[:, k:k + 2, :].rearrange("p k n -> p (k n)"), psum[:, 4 + k // 2, :],
                                        nfT_hi[:, k:k + 2, :].rearrange("p k n -> p (k n)").bitcast(F32),
                                        ALU.subtract).then_inc(hT_lo, 1)

            def low_parts(half_index, first):
                for c in range(KC):
                    dve.wait_ge(hi_ready, half_index * KC + (c + 1))
                    nc.vector.tensor_tensor(w_lo[:, c % SPLIT, :], w_raw[:, c % RAW, :],
                                            w_hi[:, c % SPLIT, :].bitcast(F32), ALU.subtract).then_inc(lo_ready, 1)

            def one_hots(t, q):
                if not (isinstance(t, int) and t < UNROLL):
                    dve.wait_ge(scatter_done, t + (1 - UNROLL))
                for end in range(2):
                    ins = nc.vector.tensor_scalar(hot[:, q, 2 + end, :], iota_row[:, :],
                                                  ids[:, end, bass.ds(t, 1)], None, ALU.is_equal)
                ins.then_inc(hot_ready, 1)

            def logits(t, q):
                b = q % 2
                dve.wait_ge(gather_done, t + 1)
                nc.vector.scalar_tensor_tensor(out=junk[:, :], in0=pz[b], scalar=0.0, in1=wa_row[:, :], op0=ALU.max,
                                               op1=ALU.mult, accum_out=logit[:, q:q + 1]).then_inc(logit_ready, 1)
                dve.wait_ge(logit_ready, t + 1)
                nc.vector.tensor_scalar(hot[:, q, 1, :], hot[:, q, 2, :].bitcast(F32), logit[:, q:q + 1], None,
                                        ALU.mult).then_inc(shi_ready, 1)
                dve.wait_ge(shi_ready, t + 1)
                nc.vector.scalar_tensor_tensor(out=hot[:, q, 0, :], in0=hot[:, q, 2, :].bitcast(F32),
                                               scalar=logit[:, q:q + 1], in1=hot[:, q, 1, :].bitcast(F32),
                                               op0=ALU.mult, op1=ALU.subtract).then_inc(scaled_ready, 1)

            for m in range(NTYPE):
                first, count = first_tile[m], tiles_of[m]
                for end in range(2):
                    s = 2 * m + end
                    low_parts(s, s == 0)
                    dve.wait_ge(bias_in, 16 * (m + 1))
                    dve.wait_ge(prod_done, s + 1)
                    if s:
                        dve.wait_ge(tb_hi, NT * s)
                    for t in range(NT):
                        made = psum[:, 4 * end + 2 * t:4 * end + 2 * t + 2, :].rearrange("p a n -> p (a n)")
                        if end:
                            ins = nc.vector.tensor_tensor(biased[:, t, :], made, bias[:, 0, :], ALU.add)
                        else:
                            ins = nc.vector.tensor_copy(biased[:, t, :], made)
                    ins.then_inc(tb_biased, 1)
                    dve.wait_ge(tb_biased, s + 1)
                    for t in range(NT):
                        dve.wait_ge(tb_hi, NT * s + t + 1)
                        nc.vector.tensor_tensor(table[:, end, t, 1, :], biased[:, t, :],
                                                table[:, end, t, 0, :].bitcast(F32), ALU.subtract).then_inc(tb_lo, 1)
                if m == 0:
                    dve.wait_ge(ids_ready, 1)
                    dve.wait_ge(small_in, 48)
                one_hots(first, first % UNROLL)

                def step_tile(t, q):
                    one_hots(t + 1, (q + 1) % UNROLL)
                    logits(t, q)
                if count > 1:
                    tiles(dve, first, count - 1, step_tile)
                logits(first + count - 1, (first + count - 1) % UNROLL)

            low_parts(2 * NTYPE, False)
            dve.wait_ge(pairs_ready, NT * NTYPE)
            total = [pairs[:, c, :, 0, :] for c in range(NT)]
            count_ = [pairs[:, c, :, 1, :] for c in range(NT)]

            def by_type(a):
                return a.rearrange("p (m n) -> p m n", m=NTYPE)
            work = [by_type(soft[:, i, :]) for i in range(3)]
            for c in range(NT):
                own(nc.vector.tensor_scalar(work[0], count_[c], 1.0, None, ALU.max))
                own(nc.vector.reciprocal(work[1], work[0]))
                own(nc.vector.tensor_tensor(work[2], total[c], work[1], ALU.mult))
                own(nc.vector.tensor_scalar(work[0], count_[c], 0.0, ABSENT, ALU.is_equal, ALU.mult))
                own(nc.vector.scalar_tensor_tensor(out=by_type(shifted[:, c, :]), in0=work[2], scalar=ba_col[:, 0:1],
                                                   in1=work[0], op0=ALU.add, op1=ALU.add))
                own(nc.vector.tensor_reduce(small[:, 0, c:c + 1], shifted[:, c, :], AX.X, ALU.max))
            nc.vector.tensor_scalar(small[:, 1, :], small[:, 0, :], -1.0, None, ALU.mult).then_inc(exp_bias, 1)
            for c in range(NT):
                dve.wait_ge(exp_done, c + 1)
                own(nc.vector.scalar_tensor_tensor(out=work[0], in0=by_type(shifted[:, c, :]), scalar=1.0,
                                                   in1=count_[c], op0=ALU.mult, op1=ALU.mult,
                                                   accum_out=small[:, 2, c:c + 1]))
                own(nc.vector.tensor_scalar(small[:, 3, c:c + 1], small[:, 2, c:c + 1], 0.5, None, ALU.max))
                own(nc.vector.reciprocal(small[:, 4, c:c + 1], small[:, 3, c:c + 1]))
                own(nc.vector.tensor_tensor(soft[:, 1, 0:N], soft[:, 0, 0:N], soft[:, 0, N:2 * N], ALU.add))
                own(nc.vector.tensor_tensor(soft[:, 2, 0:N], soft[:, 1, 0:N], soft[:, 0, 2 * N:3 * N], ALU.add))
                nc.vector.tensor_scalar(alpha[:, c, :], soft[:, 2, 0:N], small[:, 4, c:c + 1], None,
                                        ALU.mult).then_inc(alpha_ready, 1)
            for k in range(0, KC, 2):
                dve.wait_ge(z_hi, k // 2 + 1)
                nc.vector.tensor_tensor(nfT_lo[:, KC + k:KC + k + 2, :].rearrange("p k n -> p (k n)"),
                                        psum[:, 4 + k // 2, :],
                                        nfT_hi[:, KC + k:KC + k + 2, :].rearrange("p k n -> p (k n)").bitcast(F32),
                                        ALU.subtract).then_inc(z_lo, 1)

            def finish(i, rows, t, banks, n):
                if i:
                    dve.wait_ge(bias_in, 16 * (NTYPE + 1))
                dve.wait_ge(y_done, i + 1)
                own(nc.vector.tensor_tensor(junk[rows, :], psum[rows, banks:banks + 2, :].rearrange("p a n -> p (a n)"),
                                            bias[rows, 1 - i, :], ALU.add))
                nc.vector.scalar_tensor_tensor(out=out_sb[rows, t, :], in0=junk[rows, :], scalar=0.0,
                                               in1=x_sb[rows, t, :], op0=ALU.max, op1=ALU.add).then_inc(out_ready, 1)
                dve.wait_ge(out_ready, n + 1)
            low_parts(2 * NTYPE + 1, False)
            low_parts(2 * NTYPE + 2, False)
            finish(0, slice(0, n_first), 0, 2, 0)
            low_parts(2 * NTYPE + 3, False)
            finish(1, slice(n_first, P), 0, 4, 1)
            finish(1, slice(0, P), 1, 6, 2)

        @block.tensor
        def _(pe):
            pe.wait_ge(ids_f, 1)
            pe.wait_ge(consts, 4)
            for end in range(2):
                ins = nc.tensor.transpose(p_tr[0][:, end * ET:(end + 1) * ET], ids_rows[:, end, :], ident[0:ET, 0:ET])
            ins.then_inc(ids_T, 1)
            pe.wait_ge(h_ready, NT)
            for k in range(0, KC, 2):
                if k == 4:
                    pe.wait_ge(ids_ready, 1)
                for j in range(2):
                    for t in range(NT):
                        ins = nc.tensor.transpose(psum[:, 4 + k // 2, j * N + t * P:j * N + (t + 1) * P],
                                                  h_sb[:, t, (k + j) * P:(k + j + 1) * P], ident[:, :])
                ins.then_inc(hT_done, 1)
            pe.wait_ge(hT_lo, KC // 2)

            def chunk(s, c, outs, k):
                pe.wait_ge(lo_ready, s * KC + c + 1)
                for first_bank, nodes, m_rows in outs:
                    for part, w in ((nfT_hi, w_hi), (nfT_hi, w_lo), (nfT_lo, w_hi)):
                        for h in range(HALVES):
                            ins = nc.tensor.matmul(psum[0:m_rows, first_bank + h, :], part[:, k, nodes],
                                                   w[:, c % SPLIT, h * BANK:(h + 1) * BANK],
                                                   start=(outs_open[0] and part is nfT_hi and w is w_hi),
                                                   stop=(outs_close[0] and part is nfT_lo))
                ins.then_inc(chunk_used, 1)
                return ins

            outs_open, outs_close = [False], [False]

            def product(s, outs, ks):
                for c in range(KC):
                    outs_open[0] = ks[c] == 0
                    outs_close[0] = ks[c] == last_k[0]
                    chunk(s, c, outs, ks[c])

            last_k = [KC - 1]

            def transposes(t, q):
                b = q % 2
                pe.wait_ge(hot_ready, t + 1)
                if not (isinstance(t, int) and t < 2):
                    pe.wait_ge(hotT_ready, t - 1)
                for end in range(2):
                    for c in range(NT):
                        j = 2 * end + c
                        ins = nc.tensor.transpose(p_tr[b][:, j * P:(j + 1) * P].bitcast(F32R),
                                                  hot[:, q, 2 + end, c * P:(c + 1) * P], ident_r[:, :])
                ins.then_inc(tr_done, 1)

            def gather(t, q):
                b = q % 2
                pe.wait_ge(hotT_ready, t + 1)
                if not (isinstance(t, int) and t < 2):
                    pe.wait_ge(logit_ready, t - 1)
                n = 0
                for end in range(2):
                    for c in range(NT):
                        for part in range(2):
                            for h in range(HALVES):
                                ins = nc.tensor.matmul(pz[b][:, h * BANK:(h + 1) * BANK], hotT[:, b, 2 * end + c, :],
                                                       table[:, end, c, part, h * BANK:(h + 1) * BANK],
                                                       start=(n == 0), stop=(n == 7))
                            n += 1
                ins.then_inc(gather_done, 1)

            def scatter(t, q):
                pe.wait_ge(scaled_ready, t + 1)
                for c in range(NT):
                    lhs = hot[:, q, 3, c * P:(c + 1) * P]
                    nc.tensor.matmul(p_pair[c], lhs, hot[:, q, 1:3, :].rearrange("p a n -> p (a n)"),
                                     start=False, stop=False, skip_group_check=True)
                    ins = nc.tensor.matmul(p_pair[c][:, 0:N], lhs, hot[:, q, 0, :],
                                           start=False, stop=False, skip_group_check=True)
                ins.then_inc(scatter_done, 1)

            for m in range(NTYPE):
                first, count = first_tile[m], tiles_of[m]
                for end in range(2):
                    s = 2 * m + end
                    if m and end == 0:
                        pe.wait_ge(logit_ready, first)
                    if m and end == 1:
                        pe.wait_ge(pairs_ready, NT * m)
                        pe.wait_ge(hotT_ready, first)
                    product(s, [(4 * end + 2 * t, slice(t * P, (t + 1) * P), P) for t in range(NT)], list(range(KC)))
                    pe.wait_ge(chunk_used, (s + 1) * KC)
                    pe.sem_inc(prod_done, 1)
                pe.wait_ge(tb_lo, 2 * NT * (m + 1))
                for c in range(NT):
                    for i in range(BANK // N):
                        nc.tensor.matmul(p_pair[c][:, i * N:(i + 1) * N], zeros_r[:, 0:P], zeros_r[:, :],
                                         start=(i == 0), stop=False, skip_group_check=True)
                transposes(first, first % UNROLL)
                if count > 1:
                    transposes(first + 1, (first + 1) % UNROLL)
                gather(first, first % UNROLL)

                def step_tile(t, q):
                    transposes(t + 1, (q + 1) % UNROLL)
                    gather(t, q)
                    scatter(t - 1, (q - 1) % UNROLL)
                if count > 2:
                    tiles(pe, first + 1, count - 2, step_tile)
                last = first + count - 1
                if count > 1:
                    gather(last, last % UNROLL)
                    scatter(last - 1, (last - 1) % UNROLL)
                scatter(last, last % UNROLL)

            pe.wait_ge(logit_ready, ET)
            last_k[0] = 2 * KC - 1
            first_out = [(2, slice(0, n_first), n_first)]
            product(2 * NTYPE, first_out, list(range(KC)))
            pe.wait_ge(alpha_ready, NT)
            for s_tile in range(NT):
                for c in range(NT):
                    ins = nc.tensor.transpose(psum[:, 0, s_tile * N + c * P:s_tile * N + (c + 1) * P],
                                              alpha[:, c, s_tile * P:(s_tile + 1) * P], ident[:, :])
            ins.then_inc(alphaT_done, 1)
            pe.wait_ge(alphaT_ready, 1)
            pe.wait_ge(pairs_ready, NT * NTYPE)
            for k in range(KC):
                for s_tile in range(NT):
                    ins = nc.tensor.matmul(psum[:, 4 + k // 2, (k % 2) * N:(k % 2 + 1) * N],
                                           h_sb[:, s_tile, k * P:(k + 1) * P], alphaT[:, s_tile, :],
                                           start=(s_tile == 0), stop=(s_tile == NT - 1))
                if k % 2:
                    ins.then_inc(z_done, 1)
            pe.wait_ge(z_lo, KC // 2)
            product(2 * NTYPE + 1, first_out, list(range(KC, 2 * KC)))
            pe.wait_ge(chunk_used, (2 * NTYPE + 2) * KC)
            pe.sem_inc(y_done, 1)
            second_out = [(4, slice(0, P), P), (6, slice(P, N), P)]
            product(2 * NTYPE + 2, second_out, list(range(KC)))
            product(2 * NTYPE + 3, second_out, list(range(KC, 2 * KC)))
            pe.wait_ge(chunk_used, (2 * NTYPE + 4) * KC)
            pe.sem_inc(y_done, 1)


_INS = ["x", "src", "dst", "L0_gnn_W_hh", "L0_gnn_b_hh", "L0_gnn_W_oo", "L0_gnn_b_oo", "L0_gnn_W_ho", "L0_gnn_b_ho",
        "L0_gnn_W_a", "L0_gnn_b_a", "L0_gnn_W_hn", "L0_gnn_b_hn", "L0_gnn_W_on", "L0_gnn_b_on"]


def kernel(**inputs):
    import numpy as _np
    import concourse.bacc as _bacc
    from concourse import mybir as _mybir
    from concourse.bass_utils import run_bass_kernel_spmd as _run

    nc = _bacc.Bacc("TRN2", target_bir_lowering=False, num_devices=1)
    arrays, ap = {}, {}
    for name in _INS:
        a = _np.ascontiguousarray(inputs[name])
        arrays[f"in_{name}"] = a
        ap[name] = nc.dram_tensor(f"in_{name}", a.shape, _mybir.dt.from_np(a.dtype), kind="ExternalInput").ap()
    shape = tuple(inputs["x"].shape)
    out = nc.dram_tensor("out_0", shape, _mybir.dt.float32, kind="ExternalOutput").ap()
    e_hh, e_oo = 128, 640
    w = lambda n: ap[f"L0_gnn_{n}"]
    gnn_kernel(nc, ap["x"], ap["src"], ap["dst"], [w("W_hh"), w("W_oo"), w("W_ho")], [w("b_hh"), w("b_oo"), w("b_ho")],
               w("W_a"), w("b_a"), [w("W_hn"), w("W_on")], [w("b_hn"), w("b_on")], out,
               [e_hh, e_oo, inputs["src"].shape[0] - e_hh - e_oo], 64)
    r = _run(nc, [arrays], core_ids=[0])
    return r.results[0]["out_0"]
```

```python
from contextlib import ExitStack

import concourse.bass as bass
from concourse import mybir

ALU = mybir.AluOpType
ACT = mybir.ActivationFunctionType
AX = mybir.AxisListType
F32 = mybir.dt.float32
F32R = mybir.dt.float32r
I32 = mybir.dt.int32
BF16 = mybir.dt.bfloat16

P = 128
BANK = 512
EPS = 1e-5
ABSENT = -3.0e38
MAGIC = 12582912.0
RING = 4
SORTED_RING = 8
WIN = 64
GROUP = 15
RAW = 8
SPLIT = 2


def gnn_kernel(nc, x, src, dst, w_edge, b_edge, w_a, b_a, w_node, b_node, out, e_types, n_first):
    N, D = x.shape
    E = src.shape[0]
    NT = N // P
    KC = D // P
    ET = E // P
    HALVES = D // BANK
    first_tile = [sum(e_types[:i]) // P for i in range(len(e_types))]
    tiles_of = [e // P for e in e_types]
    NTYPE = len(e_types)
    NW = N // WIN
    NB = NW * NW
    CT = tiles_of[2]
    ST = CT + NB - 1
    first_sorted = first_tile[2]
    all_tiles = first_sorted + ST
    assert N == 2 * P and D == 2 * BANK and all(e % P == 0 for e in e_types)

    ctx = ExitStack()
    with ctx:
        def sb(name, shape, dt=F32):
            return ctx.enter_context(nc.sbuf_tensor(name, shape, dt))

        def sem(name):
            return ctx.enter_context(nc.semaphore(name))

        x_sb = sb("x_sb", [P, NT, D])
        h_sb = sb("h_sb", [P, NT, D])
        nfT_hi = sb("nfT_hi", [P, 2 * KC, N], F32R)
        nfT_lo = sb("nfT_lo", [P, 2 * KC, N], F32R)
        w_raw = sb("w_raw", [P, RAW, D])
        w_hi = sb("w_hi", [P, SPLIT, D], F32R)
        w_lo = sb("w_lo", [P, SPLIT, D], F32R)
        table = sb("table", [P, 2, NT, 2, D], F32R)
        biased = sb("biased", [P, NT, D])
        bias = sb("bias", [P, 2, D])
        wa_row = sb("wa_row", [P, D])
        ba_col = sb("ba_col", [P, 1])
        ids = sb("ids", [P, 2, ET])
        iota_row = sb("iota_row", [P, N])
        iota_win = sb("iota_win", [P, 2, WIN])
        numbers = sb("numbers", [P, SORTED_RING, 2])
        before = sb("before", [P, P], BF16)
        ones = sb("ones", [P, P], BF16)
        scratch = sb("scratch", [P, 2, 2304])
        ids_rows_i = scratch[0:ET, 0, 0:2 * P].rearrange("t (a e) -> t a e", a=2).bitcast(I32)
        ids_rows = scratch[0:ET, 0, 2 * P:4 * P].rearrange("t (a e) -> t a e", a=2)
        iota_i = scratch[:, 1, 0:N].bitcast(I32)
        flat = scratch[:, :, :].rearrange("p a n -> p (a n)")
        BC = NB * CT
        member = flat[:, 0:BC // 2].bitcast(BF16)
        earlier = flat[:, BC // 2:BC // 2 + BC]
        totals = flat[:, BC // 2 + BC:BC // 2 + 2 * BC]
        running = flat[:, BC // 2 + 2 * BC:BC // 2 + 3 * BC]
        upto_b = flat[:, 4352:4352 + NB * NB].rearrange("p (b c) -> p b c", b=NB)
        place = flat[:, BC // 2 + 3 * BC:BC // 2 + 4 * BC]
        spread = [flat[:, 2304 * i:2304 * i + GROUP * P // 2].bitcast(BF16).rearrange("p (t q) -> p t q", q=P)
                  for i in range(2)]
        lots = [flat[:, 2304 * i + GROUP * P // 2:2304 * i + GROUP * (P + 2 * ST) // 2].bitcast(BF16)
                .rearrange("p (t a s) -> p t a s", a=2, s=ST) for i in range(2)]
        ends = sb("ends", [P, 2, 2, CT])
        ends_tmp = place[:, 0:6 * CT].rearrange("p (i a t) -> p i a t", i=3, a=2)
        bucket = sb("bucket", [P, 5, CT])
        bucket_tmp = earlier[:, 0:3 * CT].rearrange("p (i t) -> p i t", i=3)
        by_bucket = sb("by_bucket", [P, 10, NB])
        bucketed = sb("bucketed", [P, 2, ST])
        route_b = flat[0:1, 2304:2304 + ST * NB].rearrange("p (b s) -> p b s", b=NB)
        route_f = flat[0:1, 2304 + ST * NB:2304 + ST * (NB + 7)].rearrange("p (i s) -> p i s", i=7)
        route = sb("route", [1, ST, 4], I32)
        ident = sb("ident", [P, P])
        ident_r = sb("ident_r", [P, P], F32R)
        zeros_r = sb("zeros_r", [P, P], F32R)
        hot = sb("hot", [P, RING, 4, N], F32R)
        hotT = sb("hotT", [P, 2, 4, P], F32R)
        logit = sb("logit", [P, SORTED_RING])
        stats = sb("stats", [P, 10, NT])
        pairs = sb("pairs", [P, NT, NTYPE, 2, N])
        shifted = scratch[:, 0, 0:NT * NTYPE * N].rearrange("p (c n) -> p c n", c=NT)
        alpha = scratch[:, 0, NT * NTYPE * N:NT * NTYPE * N + NT * N].rearrange("p (c n) -> p c n", c=NT)
        soft = scratch[:, 1, :].rearrange("p (i n) -> p i n", i=3)
        alphaT = scratch[:, 1, 0:NT * N].rearrange("p (c n) -> p c n", c=NT)
        small = sb("small", [P, 8, NT])
        blocks = biased[:, 1, :]
        edgeT_hi = nfT_hi[:, KC:2 * KC, :].rearrange("p k (a e) -> p (k a) e", a=2)
        edgeT_lo = nfT_lo[:, KC:2 * KC, :].rearrange("p k (a e) -> p (k a) e", a=2)
        win_table = table[:, :, :, :, :].rearrange("p a t i d -> p a (t i) d")
        sorted_hot = hot[:, :, :, :].rearrange("p q i n -> p (q i n)")[:, 0:SORTED_RING * 6 * WIN].rearrange(
            "p (q i n) -> p q i n", q=SORTED_RING, i=6)
        HIGH, DST, SRC, LOW = 0, 1, 3, 5
        out_sb = h_sb

        psum = ctx.enter_context(nc.psum_tensor("psum", [P, 8, BANK], F32))
        pz = [psum[:, 2 * b:2 * b + 2, :].rearrange("p a n -> p (a n)") for b in range(2)]
        p_pair = [psum[:, 4 + c, :] for c in range(NT)]
        p_block = psum[:, 4:6, :].rearrange("p a n -> p (a n)")
        p_tr = [psum[:, 6 + b, :] for b in range(2)]

        x_in = sem("x_in")
        ids_in = sem("ids_in")
        small_in = sem("small_in")
        bias_in = sem("bias_in")
        w_in = [sem(f"w_in{i}") for i in range(RAW)]
        consts = sem("consts")
        dve_step = sem("dve_step")
        act_step = sem("act_step")
        pool_step = sem("pool_step")
        ids_f = sem("ids_f")
        ids_T = sem("ids_T")
        ids_ready = sem("ids_ready")
        sum_ready = sem("sum_ready")
        sq_ready = sem("sq_ready")
        var_ready = sem("var_ready")
        std_ready = sem("std_ready")
        norm_ready = sem("norm_ready")
        h_ready = sem("h_ready")
        hT_done = sem("hT_done")
        hT_hi = sem("hT_hi")
        hT_lo = sem("hT_lo")
        hi_ready = sem("hi_ready")
        lo_ready = sem("lo_ready")
        chunk_used = sem("chunk_used")
        prod_done = sem("prod_done")
        tb_biased = sem("tb_biased")
        tb_hi = sem("tb_hi")
        tb_lo = sem("tb_lo")
        hot_ready = sem("hot_ready")
        tr_done = sem("tr_done")
        hotT_ready = sem("hotT_ready")
        gather_done = sem("gather_done")
        logit_ready = sem("logit_ready")
        shi_ready = sem("shi_ready")
        scaled_ready = sem("scaled_ready")
        scatter_done = sem("scatter_done")
        member_ready = sem("member_ready")
        ranks_done = sem("ranks_done")
        ranks_copied = sem("ranks_copied")
        running_ready = sem("running_ready")
        place_ready = sem("place_ready")
        lots_ready = sem("lots_ready")
        spread_ready = sem("spread_ready")
        spread_used = sem("spread_used")
        bucketed_ready = sem("bucketed_ready")
        route_ready = sem("route_ready")
        edgeT_done = sem("edgeT_done")
        edgeT_hi_ready = sem("edgeT_hi_ready")
        edgeT_ready = sem("edgeT_ready")
        biased_z = sem("biased_z")
        numbers_ready = sem("numbers_ready")
        numbers_seen = sem("numbers_seen")
        shot_ready = sem("shot_ready")
        blocks_ready = sem("blocks_ready")
        blocks_moved = sem("blocks_moved")
        pairs_ready = sem("pairs_ready")
        exp_bias = sem("exp_bias")
        exp_done = sem("exp_done")
        alpha_ready = sem("alpha_ready")
        alphaT_done = sem("alphaT_done")
        alphaT_ready = sem("alphaT_ready")
        z_done = sem("z_done")
        z_hi = sem("z_hi")
        z_lo = sem("z_lo")
        y_done = sem("y_done")
        y_biased = sem("y_biased")
        out_ready = sem("out_ready")
        out_saved = sem("out_saved")

        w_hh, w_oo, w_ho = w_edge
        w_hn, w_on = w_node
        halves = [(w_oo, 0), (w_oo, 1), (w_hh, 0), (w_hh, 1), (w_ho, 0), (w_ho, 1),
                  (w_hn, 0), (w_on, 0), (w_hn, 1), (w_on, 1)]
        OO, HH, HO, HN_H, ON_H, HN_Z, ON_Z = 0, 2, 4, 6, 7, 8, 9

        def row(v):
            return v.rearrange("(a d) -> a d", a=1).broadcast_to([P, v.shape[0]])

        def bc(a, shape, axis):
            v = a.rearrange("p (u n) -> p u n", u=1) if axis == 2 else a.rearrange("p (n u) -> p n u", u=1)
            return v.broadcast_to(shape)

        def wide(q):
            return hot[:, q, :, :]

        def tiles(eng, first, count, step):
            n = SORTED_RING
            rounds = count // n
            with eng.Fori(0, rounds) as r:
                for j in range(n):
                    step(r * n + (first + j), (first + j) % n)
            for t in range(first + rounds * n, first + count):
                step(t, t % n)

        block = ctx.enter_context(nc.Block())

        @block.sync
        def _(sp):
            sp.dma_start(x_sb[:, :, :], x.rearrange("(t p) d -> p t d", p=P)).then_inc(x_in, 16)

            def half_matrix(w, half, s):
                for c in range(KC):
                    if not (isinstance(s, int) and s * KC + c < RAW):
                        sp.wait_ge(lo_ready, s * KC + (c + 1 - RAW))
                    sp.dma_start(w_raw[:, c % RAW, :], w[bass.ds(half * D + c * P, P), :]).then_inc(w_in[c % RAW], 16)

            half_matrix(w_oo, 0, 0)
            half_matrix(w_oo, 1, 1)
            for w, s in ((w_hh, HH), (w_ho, HO)):
                with sp.Fori(0, 2) as half:
                    half_matrix(w, half, half + s)
            for s in range(HN_H, len(halves)):
                half_matrix(*halves[s], s)
            sp.wait_ge(out_ready, 1)
            sp.dma_start(out[0:n_first, :], out_sb[0:n_first, 0, :]).then_inc(out_saved, 16)
            sp.wait_ge(out_ready, 2)
            sp.dma_start(out[n_first:P, :], out_sb[n_first:P, 0, :]).then_inc(out_saved, 16)
            sp.wait_ge(out_ready, 3)
            sp.dma_start(out[P:N, :], out_sb[:, 1, :]).then_inc(out_saved, 16)
            sp.wait_ge(out_saved, 48)

        @block.gpsimd
        def _(pool):
            step = [0]

            def own(ins):
                step[0] += 1
                ins.then_inc(pool_step, 1)
                pool.wait_ge(pool_step, step[0])

            ts, tt = nc.gpsimd.tensor_scalar, nc.gpsimd.tensor_tensor
            nc.gpsimd.dma_start(ids_rows_i[:, 0, :], src.rearrange("(t e) -> t e", e=P)).then_inc(ids_in, 16)
            nc.gpsimd.dma_start(ids_rows_i[:, 1, :], dst.rearrange("(t e) -> t e", e=P)).then_inc(ids_in, 16)
            own(nc.gpsimd.memset(ident[:, :], 0.0))
            nc.gpsimd.affine_select(out=ident[:, :], in_=ident[:, :], compare_op=ALU.not_equal, fill=1.0, base=0,
                                    pattern=[[-1, P]], channel_multiplier=1).then_inc(consts, 1)
            own(nc.gpsimd.iota(iota_i, pattern=[[1, N]], base=0, channel_multiplier=0))
            nc.gpsimd.tensor_copy(iota_row[:, :], iota_i).then_inc(consts, 1)
            pool.wait_ge(consts, 2)
            nc.gpsimd.tensor_copy(ident_r[:, :], ident[:, :]).then_inc(consts, 1)
            nc.gpsimd.memset(zeros_r[:, :].bitcast(F32), 0.0).then_inc(consts, 1)
            nc.gpsimd.memset(ones[:, :], 1.0).then_inc(consts, 1)
            own(nc.gpsimd.memset(before[:, :], 1.0))
            own(nc.gpsimd.memset(upto_b, 1.0))
            nc.gpsimd.affine_select(out=upto_b, in_=upto_b, compare_op=ALU.is_ge, fill=0.0, base=0,
                                    pattern=[[1, NB], [-1, NB]], channel_multiplier=0).then_inc(consts, 1)
            nc.gpsimd.affine_select(out=before[:, :], in_=before[:, :], compare_op=ALU.is_gt, fill=0.0, base=0,
                                    pattern=[[1, P]], channel_multiplier=-1).then_inc(consts, 1)
            for i in range(2):
                own(ts(iota_win[:, i, :], iota_row[:, 0:WIN], 1.0, None, ALU.add))
            nc.gpsimd.dma_start(wa_row[:, :], row(w_a.rearrange("d a -> (d a)"))).then_inc(small_in, 16)
            nc.gpsimd.dma_start(ba_col[:, :], row(b_a)).then_inc(small_in, 16)
            nc.gpsimd.dma_start(bias[:, 1, :], row(b_node[0])).then_inc(small_in, 16)
            nc.gpsimd.dma_start(bias[:, 0, :], row(b_edge[1])).then_inc(small_in, 16)

            def whole(out_, tmp, in_, scale, shift):
                own(ts(tmp[0], in_, scale, shift, ALU.mult, ALU.add))
                own(ts(tmp[1], tmp[0], MAGIC, None, ALU.add))
                own(ts(out_, tmp[1], -MAGIC, None, ALU.add))

            def summed(out_, a):
                n = a.shape[1]
                while n > 2:
                    n //= 2
                    own(tt(a[:, 0:n, :], a[:, 0:n, :], a[:, n:2 * n, :], ALU.add))
                own(tt(out_, a[:, 0, :], a[:, 1, :], ALU.add))

            pool.wait_ge(ids_ready, 1)
            mine = ids[:, :, first_sorted:ET]
            window, number = ends[:, 0, :, :], ends[:, 1, :, :]
            whole(window, (ends_tmp[:, 0, :, :], ends_tmp[:, 1, :, :]), mine, 1.0 / WIN, 0.5 / WIN - 0.5)
            own(ts(ends_tmp[:, 2, :, :], window, -float(WIN), 1.0, ALU.mult, ALU.add))
            own(tt(number, ends_tmp[:, 2, :, :], mine, ALU.add))
            own(ts(bucket[:, 0, :], window[:, 1, :], float(NW), None, ALU.mult))
            own(tt(bucket[:, 1, :], bucket[:, 0, :], window[:, 0, :], ALU.add))
            S3 = [P, NB, CT]

            def by_b(a):
                return a.rearrange("p (b t) -> p b t", b=NB)
            for b in range(NB):
                ins = ts(by_b(member)[:, b, :], bucket[:, 1, :], float(b), None, ALU.is_equal)
            ins.then_inc(member_ready, 1)
            pool.wait_ge(ranks_copied, 2)
            pool.wait_ge(running_ready, 1)
            own(tt(running, running, totals, ALU.subtract))
            run, tot = by_b(running), by_b(totals)
            end, count, tb_, upto, first_t, base = (by_bucket[:, i, :] for i in (0, 1, 4, 5, 6, 8))
            own(tt(end, run[:, :, CT - 1], tot[:, :, CT - 1], ALU.add))
            own(tt(count, end, run[:, :, 0], ALU.subtract))
            whole(tb_, (by_bucket[:, 2, :], by_bucket[:, 3, :]), count, 1.0 / P, 0.5 - 0.5 / P)
            S2 = [P, NB, NB]
            own(tt(upto_b, upto_b, bc(tb_, S2, 2), ALU.mult))
            summed(upto, upto_b.rearrange("p b c -> p c b"))
            own(tt(first_t, upto, tb_, ALU.subtract))
            own(ts(by_bucket[:, 7, :], first_t, float(P), None, ALU.mult))
            own(tt(base, by_bucket[:, 7, :], run[:, :, 0], ALU.subtract))
            own(tt(place, earlier, running, ALU.add))
            own(tt(by_b(place), by_b(place), bc(base, S3, 1), ALU.add))
            own(tt(place, place, member, ALU.mult))
            pos, sorted_tile, slot = bucket[:, 2, :], bucket[:, 3, :], bucket[:, 4, :]
            summed(pos, by_b(place))
            whole(sorted_tile, (bucket_tmp[:, 0, :], bucket_tmp[:, 1, :]), pos, 1.0 / P, 0.5 / P - 0.5)
            own(ts(bucket_tmp[:, 2, :], sorted_tile, -float(P), None, ALU.mult))
            own(tt(slot, bucket_tmp[:, 2, :], pos, ALU.add))
            rf = [route_f[:, i, :] for i in range(7)]
            for b in range(NB):
                ins = ts(route_b[:, b, :], iota_row[0:1, 0:ST], upto[0:1, b:b + 1], None, ALU.is_ge)
            own(ins)
            summed(rf[0], route_b)
            own(ts(rf[1], rf[0], float(NB - 1), None, ALU.min))
            whole(rf[4], (rf[2], rf[3]), rf[1], 1.0 / NW, 0.5 / NW - 0.5)
            own(ts(rf[5], rf[4], -float(NW), None, ALU.mult))
            own(tt(rf[6], rf[5], rf[1], ALU.add))
            nc.gpsimd.tensor_copy(route[:, :, 0], rf[6])
            nc.gpsimd.tensor_copy(route[:, :, 1], rf[4])
            nc.gpsimd.tensor_copy(route[:, :, 2], rf[1]).then_inc(route_ready, 1)
            pool.wait_ge(route_ready, 1)
            pool.sem_inc(place_ready, 1)
            for g in range(CT // GROUP):
                i, t0 = g % 2, g * GROUP
                if g >= 2:
                    pool.wait_ge(spread_used, g - 1)

                for t in range(t0, t0 + GROUP):
                    col = slice(t, t + 1)
                    ins = ts(spread[i][:, t - t0, :], iota_row[:, 0:P], slot[:, col], None, ALU.is_equal)
                ins.then_inc(spread_ready, 1)
            pool.wait_ge(bucketed_ready, 1)

            def sorted_hots(t, q, wait=True):
                if wait:
                    pool.wait_ge(scatter_done, t + (1 - SORTED_RING))
                nc.gpsimd.tensor_copy(numbers[:, q, :], bucketed[:, :, bass.ds(t - first_sorted, 1)]
                                      .rearrange("p a u -> p (a u)")).then_inc(numbers_ready, 1)
                pool.wait_ge(numbers_ready, t + (1 - first_sorted))
                pool.sem_inc(numbers_seen, 1)
                for a, part in enumerate((DST, SRC)):
                    ins = ts(sorted_hot[:, q, part:part + 2, :], iota_win[:, :, :], numbers[:, q, a:a + 1], None, ALU.is_equal)
                ins.then_inc(shot_ready, 1)
            pool.wait_ge(scatter_done, first_sorted)
            for t in range(first_sorted, first_sorted + SORTED_RING):
                sorted_hots(t, t % SORTED_RING, False)
            tiles(pool, first_sorted + SORTED_RING, ST - SORTED_RING, sorted_hots)
            for s in (HN_H, ON_H):
                for c in range(KC):
                    pool.wait_ge(hi_ready, s * KC + (c + 1))
                    tt(w_lo[:, c % SPLIT, :], w_raw[:, c % RAW, :], w_hi[:, c % SPLIT, :].bitcast(F32),
                       ALU.subtract).then_inc(lo_ready, 1)

        @block.scalar
        def _(act):
            for t in range(NT):
                act.wait_ge(sum_ready, 1)
                nc.scalar.activation(biased[:, t, :], x_sb[:, t, :], ACT.Square, bias=stats[:, 1, t:t + 1],
                                     accum_out=stats[:, 2, t:t + 1]).then_inc(sq_ready, 1)
            act.wait_ge(var_ready, 1)
            nc.scalar.activation(stats[:, 4, :], stats[:, 3, :], ACT.Sqrt).then_inc(std_ready, 1)
            act.wait_ge(norm_ready, 1)
            for t in range(NT):
                nc.scalar.activation(h_sb[:, t, :], x_sb[:, t, :], ACT.Relu, bias=stats[:, 9, t:t + 1],
                                     scale=stats[:, 8, t:t + 1]).then_inc(h_ready, 1)

            def split4(dst_, done, ready, first_bank):
                for k in range(4):
                    act.wait_ge(done, k + 1)
                    nc.scalar.copy(dst_[:, k, :], psum[:, first_bank + k, :]).then_inc(ready, 1)
            split4(nfT_hi[:, 0:KC, :].rearrange("p (k a) n -> p k (a n)", a=2), hT_done, hT_hi, 4)

            def high_parts(s, between={}):
                for c in range(KC):
                    act.wait_ge(w_in[c % RAW], 16 * s + 16)
                    if s or c >= SPLIT:
                        act.wait_ge(chunk_used, s * KC + (c + 1 - SPLIT))
                    nc.scalar.copy(w_hi[:, c % SPLIT, :], w_raw[:, c % RAW, :]).then_inc(hi_ready, 1)
                    if c in between:
                        between[c]()

            def ranks_out():
                act.wait_ge(ranks_done, 1)
                for a, b in ((earlier, 4), (totals, 6)):
                    nc.scalar.copy(a.rearrange("p (i n) -> p i n", i=2), psum[:, b:b + 2, 0:BC // 2]).then_inc(ranks_copied, 1)

            def table_hi(i, end, t):
                act.wait_ge(tb_biased, NT * i + t + 1)
                nc.scalar.copy(table[:, end, t, 0, :], biased[:, t, :]).then_inc(tb_hi, 1)

            def win_table_hi(i, end, t, j):
                act.wait_ge(tb_biased, NT * i + t + 1)
                act.wait_ge(gather_done, first_sorted - 1)
                rows = slice(j * WIN, (j + 1) * WIN)
                nc.scalar.copy(win_table[rows, end, 2 * t + j, :], biased[rows, t, :]).then_inc(tb_hi, 1)

            def load_bias(b):
                act.dma_start(bias[:, 0, :], row(b)).then_inc(bias_in, 16)

            def pairs_out(m, upto):
                act.wait_ge(scatter_done, upto)
                for c in range(NT):
                    nc.scalar.copy(pairs[:, c, m, :, :].rearrange("p a n -> p (a n)"), p_pair[c]).then_inc(pairs_ready, 1)

            def transposed(t, b, parts=4, bank=None):
                act.wait_ge(tr_done, t + 1)
                if not isinstance(t, int) or t > 2:
                    act.wait_ge(gather_done, t - 2)
                elif t == 2:
                    act.wait_ge(edgeT_done, 4)
                nc.scalar.copy(hotT[:, b, 0:parts, :].rearrange("p c e -> p (c e)"),
                               (bank or p_tr[b])[:, 0:parts * P]).then_inc(hotT_ready, 1)

            high_parts(OO, {3: ranks_out})
            high_parts(OO + 1, {1: lambda: table_hi(0, 0, 0), 2: lambda: table_hi(0, 0, 1),
                                4: lambda: transposed(0, 0, 4, pz[0])})
            split4(edgeT_hi.rearrange("p (k a) e -> p k (a e)", a=4), edgeT_done, edgeT_hi_ready, 0)
            high_parts(HH, {1: lambda: table_hi(1, 1, 0), 2: lambda: table_hi(1, 1, 1), 3: lambda: load_bias(b_edge[0])})
            high_parts(HH + 1)
            transposed(1, 1)
            pairs_out(0, 1)
            load_bias(b_edge[2])
            for t in range(2, first_sorted):
                transposed(t, t % 2)
            pairs_out(1, first_sorted)
            high_parts(HO)
            act.wait_ge(spread_used, CT // GROUP)
            nc.scalar.copy(bucketed[:, :, :].rearrange("p a t -> p (a t)"), p_tr[0][:, 0:2 * ST]).then_inc(bucketed_ready, 1)
            high_parts(HO + 1, {1 + 2 * t + j: (lambda t=t, j=j: win_table_hi(2, 0, t, j))
                                for t in range(NT) for j in range(2)})
            for t in range(NT):
                for j in range(2):
                    win_table_hi(3, 1, t, j)
            load_bias(b_node[1])

            def scaled_hi(t, q):
                act.wait_ge(logit_ready, t + 1)
                nc.scalar.activation(sorted_hot[:, q, HIGH, :], sorted_hot[:, q, DST, :], ACT.Copy,
                                     scale=logit[:, q:q + 1]).then_inc(shi_ready, 1)

            def sorted_step(t, q):
                transposed(t + 1, (q + 1) % 2, 2)
                scaled_hi(t - 1, (q - 1) % SORTED_RING)
            f, last = first_sorted, all_tiles - 1
            transposed(f, f % 2, 2)
            transposed(f + 1, (f + 1) % 2, 2)
            tiles(act, f + 1, last - f - 1, sorted_step)
            scaled_hi(last - 1, (last - 1) % SORTED_RING)
            scaled_hi(last, last % SORTED_RING)
            act.wait_ge(scatter_done, all_tiles)
            nc.scalar.copy(blocks, p_block).then_inc(blocks_ready, 1)
            act.wait_ge(blocks_ready, 1)
            for j in range(2):
                for a in range(2):
                    act.dma_start(pairs[j * WIN:(j + 1) * WIN, :, 2, a, :],
                                  blocks[a * WIN:(a + 1) * WIN, :].rearrange("p (c j n) -> p j c n", c=NT, j=2)[:, j, :, :]
                                  ).then_inc(blocks_moved, 16)
            high_parts(HN_H)
            for c in range(NT):
                act.wait_ge(exp_bias, 1)
                nc.scalar.activation(shifted[:, c, :], shifted[:, c, :], ACT.Exp,
                                     bias=small[:, 1, c:c + 1]).then_inc(exp_done, 1)
            high_parts(ON_H)
            act.wait_ge(alphaT_done, 1)
            nc.scalar.copy(alphaT.rearrange("p c n -> p (c n)"), psum[:, 0, :]).then_inc(alphaT_ready, 1)
            for k in range(4):
                act.wait_ge(z_done, k + 1)
                nc.scalar.copy(nfT_hi[:, KC + 2 * k:KC + 2 * k + 2, :].rearrange("p k n -> p (k n)"),
                               psum[:, k % 2, :]).then_inc(z_hi, 1)
            high_parts(HN_Z)
            high_parts(ON_Z)

        @block.vector
        def _(dve):
            step = [0]

            def own(ins):
                step[0] += 1
                ins.then_inc(dve_step, 1)
                dve.wait_ge(dve_step, step[0])

            dve.wait_ge(ids_in, 32)
            nc.vector.tensor_copy(ids_rows, ids_rows_i).then_inc(ids_f, 1)
            dve.wait_ge(x_in, 16)
            own(nc.vector.tensor_reduce(stats[:, 0, :], x_sb[:, :, :], AX.X, ALU.add))
            nc.vector.tensor_scalar(stats[:, 1, :], stats[:, 0, :], -1.0 / D, None, ALU.mult).then_inc(sum_ready, 1)
            dve.wait_ge(ids_T, 1)
            nc.vector.tensor_copy(ids[:, :, :], p_tr[0][:, 0:2 * ET].rearrange("p (a t) -> p a t", a=2)).then_inc(ids_ready, 1)
            dve.wait_ge(sq_ready, NT)
            nc.vector.tensor_scalar(stats[:, 3, :], stats[:, 2, :], 1.0 / D, EPS, ALU.mult, ALU.add).then_inc(var_ready, 1)
            dve.wait_ge(std_ready, 1)
            own(nc.vector.reciprocal(stats[:, 5, :], stats[:, 4, :]))
            own(nc.vector.tensor_tensor(stats[:, 6, :], stats[:, 5, :], stats[:, 5, :], ALU.mult))
            own(nc.vector.tensor_tensor(stats[:, 7, :], stats[:, 6, :], stats[:, 3, :], ALU.mult))
            own(nc.vector.tensor_scalar(stats[:, 6, :], stats[:, 7, :], -0.5, 1.5, ALU.mult, ALU.add))
            own(nc.vector.tensor_tensor(stats[:, 8, :], stats[:, 5, :], stats[:, 6, :], ALU.mult))
            nc.vector.tensor_tensor(stats[:, 9, :], stats[:, 8, :], stats[:, 1, :], ALU.mult).then_inc(norm_ready, 1)

            def split4(dst_lo, dst_hi, hi, ready, first_bank):
                for k in range(4):
                    dve.wait_ge(hi, k + 1)
                    nc.vector.tensor_tensor(dst_lo[:, k, :], psum[:, first_bank + k, :], dst_hi[:, k, :].bitcast(F32),
                                            ALU.subtract).then_inc(ready, 1)
            split4(nfT_lo[:, 0:KC, :].rearrange("p (k a) n -> p k (a n)", a=2),
                   nfT_hi[:, 0:KC, :].rearrange("p (k a) n -> p k (a n)", a=2), hT_hi, hT_lo, 4)

            def low_parts(s, between={}):
                for c in range(KC):
                    dve.wait_ge(hi_ready, s * KC + (c + 1))
                    nc.vector.tensor_tensor(w_lo[:, c % SPLIT, :], w_raw[:, c % RAW, :],
                                            w_hi[:, c % SPLIT, :].bitcast(F32), ALU.subtract).then_inc(lo_ready, 1)
                    if c in between:
                        between[c]()

            def one_hots(t, q):
                if t >= RING:
                    dve.wait_ge(scatter_done, t + (1 - RING))
                for end in range(2):
                    ins = nc.vector.tensor_scalar(wide(q)[:, 2 + end, :], iota_row[:, :], ids[:, end, t:t + 1], None,
                                                  ALU.is_equal)
                ins.then_inc(hot_ready, 1)

            def weighted_sum(z, q):
                nc.vector.scalar_tensor_tensor(out=biased[:, q % 2, :], in0=z, scalar=0.0, in1=wa_row[:, :], op0=ALU.max,
                                               op1=ALU.mult, accum_out=logit[:, q:q + 1]).then_inc(logit_ready, 1)

            def scaled(t, q):
                dve.wait_ge(logit_ready, t + 1)
                nc.vector.tensor_scalar(wide(q)[:, 1, :], wide(q)[:, 2, :].bitcast(F32), logit[:, q:q + 1], None,
                                        ALU.mult).then_inc(shi_ready, 1)
                dve.wait_ge(shi_ready, t + 1)
                nc.vector.scalar_tensor_tensor(out=wide(q)[:, 0, :], in0=wide(q)[:, 2, :].bitcast(F32),
                                               scalar=logit[:, q:q + 1], in1=wide(q)[:, 1, :].bitcast(F32),
                                               op0=ALU.mult, op1=ALU.subtract).then_inc(scaled_ready, 1)

            def with_bias(i, s, end, t, loads=0):
                if end and t == 0:
                    dve.wait_ge(*((bias_in, 16 * loads) if loads else (small_in, 64)))
                dve.wait_ge(chunk_used, (s + 1) * KC)
                if i:
                    dve.wait_ge(tb_hi, (2, 4, 8)[i - 1])
                made = psum[:, 4 * end + 2 * t:4 * end + 2 * t + 2, :].rearrange("p a n -> p (a n)")
                if end:
                    ins = nc.vector.tensor_tensor(biased[:, t, :], made, bias[:, 0, :], ALU.add)
                else:
                    ins = nc.vector.tensor_copy(biased[:, t, :], made)
                ins.then_inc(tb_biased, 1)

            def table_lo(i, end, t):
                dve.wait_ge(tb_hi, NT * i + t + 1)
                nc.vector.tensor_tensor(table[:, end, t, 1, :], biased[:, t, :],
                                        table[:, end, t, 0, :].bitcast(F32), ALU.subtract).then_inc(tb_lo, 1)

            def win_table_lo(i, end, t, j):
                dve.wait_ge(tb_hi, 4 * (i - 1) + 2 * t + j + 1)
                rows, other = slice(j * WIN, (j + 1) * WIN), slice((1 - j) * WIN, (2 - j) * WIN)
                nc.vector.tensor_tensor(win_table[other, end, 2 * t + j, :], biased[rows, t, :],
                                        win_table[rows, end, 2 * t + j, :].bitcast(F32),
                                        ALU.subtract).then_inc(tb_lo, 1)

            def running_sums():
                dve.wait_ge(ranks_copied, 2)
                nc.vector.tensor_tensor_scan(running, totals, totals, 0.0, ALU.add, ALU.bypass).then_inc(running_ready, 1)

            def lots_group(g):
                if g == 0:
                    dve.wait_ge(place_ready, 1)
                if g >= 2:
                    dve.wait_ge(spread_used, g - 1)
                with dve.Fori(0, GROUP) as t:
                    col = bass.ds(t + g * GROUP, 1)
                    for a, end in enumerate((1, 0)):
                        nc.vector.tensor_scalar(lots[g % 2][:, bass.ds(t, 1), a, :].rearrange("p u s -> p (u s)"),
                                                iota_row[:, 0:ST], bucket[:, 3, col], ends[:, 1, end, col],
                                                ALU.is_equal, ALU.mult).then_inc(lots_ready, 1)

            dve.wait_ge(consts, 2)
            one_hots(0, 0)
            low_parts(OO, {4: running_sums})
            low_parts(OO + 1, {0: lambda: with_bias(0, OO, 0, 0), 1: lambda: with_bias(0, OO, 0, 1),
                               2: lambda: table_lo(0, 0, 0), 3: lambda: table_lo(0, 0, 1)})
            split4(edgeT_lo.rearrange("p (k a) e -> p k (a e)", a=4), edgeT_hi.rearrange("p (k a) e -> p k (a e)", a=4),
                   edgeT_hi_ready, edgeT_ready, 0)
            low_parts(HH, {0: lambda: with_bias(1, OO + 1, 1, 0), 1: lambda: with_bias(1, OO + 1, 1, 1),
                           2: lambda: table_lo(1, 1, 0), 3: lambda: table_lo(1, 1, 1)})
            low_parts(HH + 1)
            one_hots(1, 1)
            dve.wait_ge(bias_in, 16)
            dve.wait_ge(chunk_used, (HH + 2) * KC)
            nc.vector.tensor_tensor(biased[:, 1, :], pz[0], bias[:, 0, :], ALU.add).then_inc(biased_z, 1)
            dve.wait_ge(biased_z, 1)
            weighted_sum(biased[:, 1, :], 0)
            scaled(0, 0)
            for t in range(1, first_sorted):
                if t + 1 < first_sorted:
                    one_hots(t + 1, (t + 1) % RING)
                dve.wait_ge(gather_done, t)
                weighted_sum(pz[t % 2], t % RING)
                scaled(t, t % RING)
            lots_group(0)
            low_parts(HO, {2 * g - 1: (lambda g=g: lots_group(g)) for g in range(1, CT // GROUP)})
            between = {0: lambda: with_bias(2, HO, 0, 0), 1: lambda: with_bias(2, HO, 0, 1)}
            between |= {2 + 2 * t + j: (lambda t=t, j=j: win_table_lo(2, 0, t, j)) for t in range(NT) for j in range(2)}
            low_parts(HO + 1, between)
            for t in range(NT):
                with_bias(3, HO + 1, 1, t, 2)
            for t in range(NT):
                for j in range(2):
                    win_table_lo(3, 1, t, j)

            def sorted_logit(t, q):
                dve.wait_ge(gather_done, t)
                weighted_sum(pz[q % 2], q)

            def scaled_lo(t, q):
                dve.wait_ge(shi_ready, t + 1)
                nc.vector.scalar_tensor_tensor(out=sorted_hot[:, q, LOW, :], in0=sorted_hot[:, q, DST, :].bitcast(F32),
                                               scalar=logit[:, q:q + 1], in1=sorted_hot[:, q, HIGH, :].bitcast(F32),
                                               op0=ALU.mult, op1=ALU.subtract).then_inc(scaled_ready, 1)

            def sorted_step(t, q):
                sorted_logit(t, q)
                scaled_lo(t - 1, (q - 1) % SORTED_RING)
            f, last = first_sorted, all_tiles - 1
            sorted_logit(f, f % SORTED_RING)
            tiles(dve, f + 1, last - f, sorted_step)
            scaled_lo(last, last % SORTED_RING)

            dve.wait_ge(pairs_ready, NT * 2)
            dve.wait_ge(blocks_moved, 64)
            total = [pairs[:, c, :, 0, :] for c in range(NT)]
            count_ = [pairs[:, c, :, 1, :] for c in range(NT)]

            def by_type(a):
                return a.rearrange("p (m n) -> p m n", m=NTYPE)
            work = [by_type(soft[:, i, :]) for i in range(3)]
            for c in range(NT):
                own(nc.vector.tensor_scalar(work[0], count_[c], 1.0, None, ALU.max))
                own(nc.vector.reciprocal(work[1], work[0]))
                own(nc.vector.tensor_tensor(work[2], total[c], work[1], ALU.mult))
                own(nc.vector.tensor_scalar(work[0], count_[c], 0.0, ABSENT, ALU.is_equal, ALU.mult))
                own(nc.vector.scalar_tensor_tensor(out=by_type(shifted[:, c, :]), in0=work[2], scalar=ba_col[:, 0:1],
                                                   in1=work[0], op0=ALU.add, op1=ALU.add))
                own(nc.vector.tensor_reduce(small[:, 0, c:c + 1], shifted[:, c, :], AX.X, ALU.max))
            nc.vector.tensor_scalar(small[:, 1, :], small[:, 0, :], -1.0, None, ALU.mult).then_inc(exp_bias, 1)
            for c in range(NT):
                dve.wait_ge(exp_done, c + 1)
                own(nc.vector.scalar_tensor_tensor(out=work[0], in0=by_type(shifted[:, c, :]), scalar=1.0,
                                                   in1=count_[c], op0=ALU.mult, op1=ALU.mult,
                                                   accum_out=small[:, 2, c:c + 1]))
                own(nc.vector.tensor_scalar(small[:, 3, c:c + 1], small[:, 2, c:c + 1], 0.5, None, ALU.max))
                own(nc.vector.reciprocal(small[:, 4, c:c + 1], small[:, 3, c:c + 1]))
                own(nc.vector.tensor_tensor(soft[:, 1, 0:N], soft[:, 0, 0:N], soft[:, 0, N:2 * N], ALU.add))
                own(nc.vector.tensor_tensor(soft[:, 2, 0:N], soft[:, 1, 0:N], soft[:, 0, 2 * N:3 * N], ALU.add))
                nc.vector.tensor_scalar(alpha[:, c, :], soft[:, 2, 0:N], small[:, 4, c:c + 1], None,
                                        ALU.mult).then_inc(alpha_ready, 1)
            for k in range(4):
                dve.wait_ge(z_hi, k + 1)
                two = slice(KC + 2 * k, KC + 2 * k + 2)
                nc.vector.tensor_tensor(nfT_lo[:, two, :].rearrange("p k n -> p (k n)"), psum[:, k % 2, :],
                                        nfT_hi[:, two, :].rearrange("p k n -> p (k n)").bitcast(F32),
                                        ALU.subtract).then_inc(z_lo, 1)
            low_parts(HN_Z)

            def finish(i, s, rows, t, bank, n):
                dve.wait_ge(chunk_used, (s + 1) * KC)
                own(nc.vector.tensor_tensor(biased[rows, t, :], psum[rows, bank:bank + 2, :].rearrange("p a n -> p (a n)"),
                                            bias[rows, 1 - i, :], ALU.add))
                nc.vector.scalar_tensor_tensor(out=out_sb[rows, t, :], in0=biased[rows, t, :], scalar=0.0,
                                               in1=x_sb[rows, t, :], op0=ALU.max, op1=ALU.add).then_inc(out_ready, 1)
            finish(0, HN_Z, slice(0, n_first), 0, 2, 0)
            low_parts(ON_Z)
            dve.wait_ge(bias_in, 48)
            finish(1, ON_Z, slice(n_first, P), 0, 4, 1)
            finish(1, ON_Z, slice(0, P), 1, 6, 2)

        @block.tensor
        def _(pe):
            pe.wait_ge(ids_f, 1)
            pe.wait_ge(consts, 7)
            for end in range(2):
                ins = nc.tensor.transpose(p_tr[0][:, end * ET:(end + 1) * ET], ids_rows[:, end, :], ident[0:ET, 0:ET])
            ins.then_inc(ids_T, 1)
            pe.wait_ge(h_ready, NT)
            for k in range(0, KC, 2):
                if k == 4:
                    pe.wait_ge(ids_ready, 1)
                for j in range(2):
                    for t in range(NT):
                        ins = nc.tensor.transpose(psum[:, 4 + k // 2, j * N + t * P:j * N + (t + 1) * P],
                                                  h_sb[:, t, (k + j) * P:(k + j + 1) * P], ident[:, :])
                ins.then_inc(hT_done, 1)
            pe.wait_ge(hT_lo, 4)

            def product(s, outs, hi, lo, k0, opens, closes, between={}):
                for c in range(KC):
                    pe.wait_ge(lo_ready, s * KC + c + 1)
                    for first_bank, cols in outs:
                        m_rows = cols.stop - cols.start
                        for n, (part, w) in enumerate(((hi, w_hi), (hi, w_lo), (lo, w_hi))):
                            for h in range(HALVES):
                                ins = nc.tensor.matmul(psum[0:m_rows, first_bank + h, :], part[:, k0 + c, cols],
                                                       w[:, c % SPLIT, h * BANK:(h + 1) * BANK],
                                                       start=(opens and c == 0 and n == 0),
                                                       stop=(closes and c == KC - 1 and n == 2))
                    ins.then_inc(chunk_used, 1)
                    if c in between:
                        between[c]()

            node_tiles = [slice(t * P, (t + 1) * P) for t in range(NT)]

            def products_of(s, end, between={}):
                product(s, [(4 * end + 2 * t, node_tiles[t]) for t in range(NT)], nfT_hi, nfT_lo, 0, True, True, between)

            def ranks():
                pe.wait_ge(member_ready, 1)
                for b, m in ((4, before), (6, ones)):
                    for h in range(2):
                        ins = nc.tensor.matmul(psum[:, b + h, 0:BC // 2], m[:, :], member[:, h * BC // 2:(h + 1) * BC // 2],
                                               start=True, stop=True)
                ins.then_inc(ranks_done, 1)

            def spread_group(g):
                pe.wait_ge(spread_ready, g + 1)
                pe.wait_ge(lots_ready, 2 * GROUP * (g + 1))
                if g == 0:
                    pe.wait_ge(hotT_ready, first_sorted)
                for t in range(GROUP):
                    ins = nc.tensor.matmul(p_tr[0][:, 0:2 * ST], spread[g % 2][:, t, :],
                                           lots[g % 2][:, t, :, :].rearrange("p a s -> p (a s)"),
                                           start=(g == 0 and t == 0), stop=(g == CT // GROUP - 1 and t == GROUP - 1),
                                           skip_group_check=True)
                ins.then_inc(spread_used, 1)

            def open_pairs():
                for c in range(NT):
                    for i in range(BANK // P):
                        nc.tensor.matmul(p_pair[c][:, i * P:(i + 1) * P], zeros_r[:, :], zeros_r[:, :],
                                         start=(i == 0), stop=False, skip_group_check=True)

            def transposes(t, q, bank=None):
                b = q % 2
                pe.wait_ge(hot_ready, t + 1)
                if t >= 2:
                    pe.wait_ge(hotT_ready, t - 1)
                for end in range(2):
                    for c in range(NT):
                        j = 2 * end + c
                        ins = nc.tensor.transpose((bank or p_tr[b])[:, j * P:(j + 1) * P].bitcast(F32R),
                                                  wide(q)[:, 2 + end, c * P:(c + 1) * P], ident_r[:, :])
                ins.then_inc(tr_done, 1)

            def gather(t, q):
                b = q % 2
                pe.wait_ge(hotT_ready, t + 1)
                if t >= 2:
                    pe.wait_ge(logit_ready, t - 1)
                n = 0
                for end in range(2):
                    for c in range(NT):
                        for part in range(2):
                            for h in range(HALVES):
                                ins = nc.tensor.matmul(pz[b][:, h * BANK:(h + 1) * BANK], hotT[:, b, 2 * end + c, :],
                                                       table[:, end, c, part, h * BANK:(h + 1) * BANK],
                                                       start=(n == 0), stop=(n == 7))
                            n += 1
                ins.then_inc(gather_done, 1)

            def scatter(t, q):
                pe.wait_ge(scaled_ready, t + 1)
                for c in range(NT):
                    lhs = wide(q)[:, 3, c * P:(c + 1) * P]
                    nc.tensor.matmul(p_pair[c], lhs, wide(q)[:, 1:3, :].rearrange("p a n -> p (a n)"),
                                     start=False, stop=False, skip_group_check=True)
                    ins = nc.tensor.matmul(p_pair[c][:, 0:N], lhs, wide(q)[:, 0, :],
                                           start=False, stop=False, skip_group_check=True)
                ins.then_inc(scatter_done, 1)

            def first_transposes():
                pe.wait_ge(tb_biased, NT)
                transposes(0, 0, pz[0])

            def edge_features():
                pe.wait_ge(hotT_ready, 1)
                for j in range(2 * KC):
                    end, k = j // KC, j % KC
                    for t in range(NT):
                        ins = nc.tensor.matmul(psum[:, j // 4, (j % 4) * P:(j % 4 + 1) * P],
                                               h_sb[:, t, k * P:(k + 1) * P], hotT[:, 0, 2 * end + t, :].bitcast(F32),
                                               start=(t == 0), stop=(t == NT - 1))
                    if j % 4 == 3:
                        ins.then_inc(edgeT_done, 1)

            products_of(OO, 0, {1: ranks})
            pe.wait_ge(ranks_copied, 2)
            products_of(OO + 1, 1, {3: first_transposes, 5: edge_features})
            pe.wait_ge(edgeT_ready, 4)
            edges = [(0, slice(0, P))]
            product(HH, edges, edgeT_hi, edgeT_lo, 0, True, False)
            product(HH + 1, edges, edgeT_hi, edgeT_lo, KC, False, True)
            pe.wait_ge(tb_biased, 2 * NT)
            open_pairs()
            transposes(1, 1)
            pe.wait_ge(tb_lo, 4)
            gather(1, 1)
            scatter(0, 0)
            transposes(2, 2)
            gather(2, 2)
            pe.wait_ge(pairs_ready, NT)
            open_pairs()
            for t in range(3, first_sorted):
                transposes(t, t % RING)
                gather(t, t % RING)
                scatter(t - 2, (t - 2) % RING)
            scatter(first_sorted - 2, (first_sorted - 2) % RING)
            scatter(first_sorted - 1, (first_sorted - 1) % RING)

            pe.wait_ge(logit_ready, first_sorted)
            products_of(HO, 0, {1 + 2 * g: (lambda g=g: spread_group(g)) for g in range(CT // GROUP)})
            pe.wait_ge(pairs_ready, 2 * NT)
            pe.wait_ge(bucketed_ready, 1)
            products_of(HO + 1, 1)
            pe.wait_ge(tb_lo, 12)
            open_pairs()
            pe.wait_ge(route_ready, 1)

            def load(t, a, b):
                _, vals = nc.values_load_multi_w_load_instructions(
                    route[0:1, bass.ds(t - first_sorted, 1), a:b].rearrange("p u n -> p (u n)"),
                    engines=[mybir.EngineType.PE], min_val=0, max_val=NW - 1 if a == 0 else NB - 1,
                    skip_runtime_bounds_check_because="the sort clamps them")
                return vals

            def sorted_transposes(t, q):
                b = q % 2
                pe.wait_ge(shot_ready, t + (1 - first_sorted))
                pe.wait_ge(hotT_ready, t - 1)
                for j, part in enumerate((DST, SRC)):
                    twice = sorted_hot[:, q, part:part + 2, :].rearrange("p i n -> p (i n)")
                    ins = nc.tensor.transpose(p_tr[b][:, j * P:(j + 1) * P].bitcast(F32R), twice, ident_r[:, :])
                ins.then_inc(tr_done, 1)

            def sorted_gather(t, q):
                b = q % 2
                w_src, w_dst = load(t, 0, 2)
                pe.wait_ge(hotT_ready, t + 1)
                pe.wait_ge(logit_ready, t - 1)
                for j, (end, w) in enumerate(((1, w_dst), (0, w_src))):
                    for h in range(HALVES):
                        rows = win_table[:, end, bass.ds(w, 1), h * BANK:(h + 1) * BANK].rearrange("p u n -> p (u n)")
                        ins = nc.tensor.matmul(pz[b][:, h * BANK:(h + 1) * BANK], hotT[:, b, j, :], rows,
                                               start=(j == 0), stop=(j == 1))
                ins.then_inc(gather_done, 1)

            def sorted_scatter(t, q):
                (bk,) = load(t, 2, 3)
                pe.wait_ge(scaled_ready, t + 1)
                to = bass.ds(bk * WIN, WIN)
                nc.tensor.matmul(p_block[:, to], sorted_hot[:, q, HIGH:DST + 1, :].rearrange("p i n -> p (i n)"),
                                 sorted_hot[:, q, SRC, :], start=False, stop=False, skip_group_check=True)
                nc.tensor.matmul(p_block[0:WIN, to], sorted_hot[:, q, LOW, :], sorted_hot[:, q, SRC, :],
                                 start=False, stop=False, skip_group_check=True).then_inc(scatter_done, 1)

            def sorted_step(t, q):
                sorted_transposes(t + 1, (q + 1) % SORTED_RING)
                sorted_gather(t, q)
                sorted_scatter(t - 2, (q - 2) % SORTED_RING)
            f, last = first_sorted, all_tiles - 1
            sorted_transposes(f, f % SORTED_RING)
            for t in (f, f + 1):
                sorted_transposes(t + 1, (t + 1) % SORTED_RING)
                sorted_gather(t, t % SORTED_RING)
            tiles(pe, f + 2, last - f - 2, sorted_step)
            sorted_gather(last, last % SORTED_RING)
            for t in (last - 2, last - 1, last):
                sorted_scatter(t, t % SORTED_RING)

            pe.wait_ge(logit_ready, all_tiles)
            first_out = [(2, slice(0, n_first))]
            second_out = [(4 + 2 * t, node_tiles[t]) for t in range(NT)]
            product(HN_H, first_out, nfT_hi, nfT_lo, 0, True, False)
            pe.wait_ge(blocks_ready, 1)
            product(ON_H, second_out, nfT_hi, nfT_lo, 0, True, False)
            pe.wait_ge(alpha_ready, NT)
            for s_tile in range(NT):
                for c in range(NT):
                    ins = nc.tensor.transpose(psum[:, 0, s_tile * N + c * P:s_tile * N + (c + 1) * P],
                                              alpha[:, c, s_tile * P:(s_tile + 1) * P], ident[:, :])
            ins.then_inc(alphaT_done, 1)
            pe.wait_ge(alphaT_ready, 1)
            for k in range(KC):
                if k in (4, 6):
                    pe.wait_ge(z_lo, k // 2 - 1)
                for s_tile in range(NT):
                    ins = nc.tensor.matmul(psum[:, (k // 2) % 2, (k % 2) * N:(k % 2 + 1) * N],
                                           h_sb[:, s_tile, k * P:(k + 1) * P], alphaT[:, s_tile, :],
                                           start=(s_tile == 0), stop=(s_tile == NT - 1))
                if k % 2:
                    ins.then_inc(z_done, 1)
            pe.wait_ge(z_lo, 4)
            product(HN_Z, first_out, nfT_hi, nfT_lo, KC, False, True)
            product(ON_Z, second_out, nfT_hi, nfT_lo, KC, False, True)


_INS = ["x", "src", "dst", "L0_gnn_W_hh", "L0_gnn_b_hh", "L0_gnn_W_oo", "L0_gnn_b_oo", "L0_gnn_W_ho", "L0_gnn_b_ho",
        "L0_gnn_W_a", "L0_gnn_b_a", "L0_gnn_W_hn", "L0_gnn_b_hn", "L0_gnn_W_on", "L0_gnn_b_on"]


def kernel(**inputs):
    import numpy as _np
    import concourse.bacc as _bacc
    from concourse import mybir as _mybir
    from concourse.bass_utils import run_bass_kernel_spmd as _run

    nc = _bacc.Bacc("TRN2", target_bir_lowering=False, num_devices=1)
    arrays, ap = {}, {}
    for name in _INS:
        a = _np.ascontiguousarray(inputs[name])
        arrays[f"in_{name}"] = a
        ap[name] = nc.dram_tensor(f"in_{name}", a.shape, _mybir.dt.from_np(a.dtype), kind="ExternalInput").ap()
    shape = tuple(inputs["x"].shape)
    out = nc.dram_tensor("out_0", shape, _mybir.dt.float32, kind="ExternalOutput").ap()
    e_hh, e_oo = 128, 640
    w = lambda n: ap[f"L0_gnn_{n}"]
    gnn_kernel(nc, ap["x"], ap["src"], ap["dst"], [w("W_hh"), w("W_oo"), w("W_ho")], [w("b_hh"), w("b_oo"), w("b_ho")],
               w("W_a"), w("b_a"), [w("W_hn"), w("W_on")], [w("b_hn"), w("b_on")], out,
               [e_hh, e_oo, inputs["src"].shape[0] - e_hh - e_oo], 64)
    r = _run(nc, [arrays], core_ids=[0])
    return r.results[0]["out_0"]
```

```python
from contextlib import ExitStack

import concourse.bass as bass
from concourse import mybir

ALU = mybir.AluOpType
ACT = mybir.ActivationFunctionType
AX = mybir.AxisListType
F32 = mybir.dt.float32
F32R = mybir.dt.float32r
I32 = mybir.dt.int32
BF16 = mybir.dt.bfloat16

P = 128
BANK = 512
EPS = 1e-5
ABSENT = -3.0e38
MAGIC = 12582912.0
RING = 4
SORTED_RING = 10
WIN = 64
GROUP = 15
RAW = 8
SPLIT = 3


def gnn_kernel(nc, x, src, dst, w_edge, b_edge, w_a, b_a, w_node, b_node, out, e_types, n_first):
    N, D = x.shape
    E = src.shape[0]
    NT = N // P
    KC = D // P
    ET = E // P
    HALVES = D // BANK
    first_tile = [sum(e_types[:i]) // P for i in range(len(e_types))]
    tiles_of = [e // P for e in e_types]
    NTYPE = len(e_types)
    NW = N // WIN
    NB = NW * NW
    CT = tiles_of[2]
    ST = CT + NB - 1
    first_sorted = first_tile[2]
    all_tiles = first_sorted + ST
    assert N == 2 * P and D == 2 * BANK and n_first == WIN and all(e % P == 0 for e in e_types)

    ctx = ExitStack()
    with ctx:
        def sb(name, shape, dt=F32):
            return ctx.enter_context(nc.sbuf_tensor(name, shape, dt))

        def sem(name):
            return ctx.enter_context(nc.semaphore(name))

        h_sb = sb("h_sb", [P, NT, D])
        nfT_hi = sb("nfT_hi", [P, 2 * KC, N], F32R)
        nfT_lo = sb("nfT_lo", [P, 2 * KC, N], F32R)
        w_raw = sb("w_raw", [P, RAW, D])
        w_hi = sb("w_hi", [P, SPLIT, D], F32R)
        w_lo = sb("w_lo", [P, SPLIT, D], F32R)
        table = sb("table", [P, 2, NT, 2, D], F32R)
        biased = sb("biased", [P, NT, D])
        bias = sb("bias", [P, 2, D])
        wa_row = sb("wa_row", [P, D])
        ba_col = sb("ba_col", [P, 1])
        ids = sb("ids", [P, 2, ET])
        iota_row = sb("iota_row", [P, N])
        iota_win = sb("iota_win", [P, 2, WIN])
        numbers = sb("numbers", [P, SORTED_RING, 2])
        iota_half = sb("iota_half", [P, P], BF16)
        before = sb("before", [P, P], BF16)
        ones = sb("ones", [P, P], BF16)
        scratch = sb("scratch", [P, 2, 2304])
        ids_rows_i = scratch[0:ET, 0, 0:2 * P].rearrange("t (a e) -> t a e", a=2).bitcast(I32)
        ids_rows = scratch[0:ET, 0, 2 * P:4 * P].rearrange("t (a e) -> t a e", a=2)
        iota_i = scratch[:, 1, 0:N].bitcast(I32)
        flat = scratch[:, :, :].rearrange("p a n -> p (a n)")
        BC = NB * CT
        member = flat[:, 0:BC // 2].bitcast(BF16)
        earlier = flat[:, BC // 2:BC // 2 + BC]
        totals = flat[:, BC // 2 + BC:BC // 2 + 2 * BC]
        running = flat[:, BC // 2 + 2 * BC:BC // 2 + 3 * BC]
        upto_b = flat[:, 4352:4352 + NB * NB].rearrange("p (b c) -> p b c", b=NB)
        place = flat[:, BC // 2 + 3 * BC:BC // 2 + 4 * BC]
        spread = [flat[:, 2304 * i:2304 * i + GROUP * P // 2].bitcast(BF16).rearrange("p (t q) -> p t q", q=P)
                  for i in range(2)]
        lots = [flat[:, 2304 * i + GROUP * P // 2:2304 * i + GROUP * (P + 2 * ST) // 2].bitcast(BF16)
                .rearrange("p (t a s) -> p t a s", a=2, s=ST) for i in range(2)]
        ends = sb("ends", [P, 2, 2, CT])
        ends_tmp = place[:, 0:6 * CT].rearrange("p (i a t) -> p i a t", i=3, a=2)
        bucket = sb("bucket", [P, 5, CT])
        bucket_tmp = earlier[:, 0:3 * CT].rearrange("p (i t) -> p i t", i=3)
        by_bucket = sb("by_bucket", [P, 10, NB])
        bucketed = sb("bucketed", [P, 2, ST])
        route = sb("route", [1, ST, 3], I32)
        ident = sb("ident", [P, P])
        ident_r = sb("ident_r", [P, P], F32R)
        zeros_r = sb("zeros_r", [P, P], F32R)
        hot = sb("hot", [P, RING, 4, N], F32R)
        hotT = sb("hotT", [P, 2, 4, P], F32R)
        logit = sb("logit", [P, SORTED_RING])
        stats = sb("stats", [P, 10, NT])
        pairs = sb("pairs", [P, NT, NTYPE, 2, N])
        shifted = scratch[:, 0, 0:NT * NTYPE * N].rearrange("p (c n) -> p c n", c=NT)
        alpha = scratch[:, 0, NT * NTYPE * N:NT * NTYPE * N + NT * N].rearrange("p (c n) -> p c n", c=NT)
        soft = scratch[:, 1, :].rearrange("p (i n) -> p i n", i=3)
        alphaT = scratch[:, 1, 0:NT * N].rearrange("p (c n) -> p c n", c=NT)
        small = sb("small", [P, 8, NT])
        pairs_flat = pairs[:, :, :, :, :].rearrange("p c m a n -> p (c m a n)")
        route_b = pairs_flat[0:1, 0:ST * NB].rearrange("p (b s) -> p b s", b=NB)
        route_f = pairs_flat[0:1, ST * NB:ST * (NB + 7)].rearrange("p (i s) -> p i s", i=7)
        x_sb = pairs_flat[:, 0:NT * D].rearrange("p (t d) -> p t d", t=NT)
        blocks = scratch[:, 1, 0:D]
        edgeT_hi = nfT_hi[:, KC:2 * KC, :].rearrange("p k (a e) -> p (k a) e", a=2)
        edgeT_lo = nfT_lo[:, KC:2 * KC, :].rearrange("p k (a e) -> p (k a) e", a=2)
        packed = nfT_hi[:, KC:2 * KC, :].rearrange("p k (q n) -> p k q n", q=4)
        z1 = nfT_lo[:, KC:2 * KC, :].rearrange("p k (i n) -> p k i n", i=2)
        win_table = table[:, :, :, :, :].rearrange("p a t i d -> p a (t i) d")
        win_rows = table[:, :, :, :, :].rearrange("p a t i d -> p (a t i d)")
        sorted_hot = hot[:, :, :, :].rearrange("p q i n -> p (q i n)")[:, 0:SORTED_RING * 4 * WIN].rearrange(
            "p (q i n) -> p q i n", q=SORTED_RING, i=4)
        DST, SRC = 0, 2
        added = flat[:, NT * NTYPE * N:NT * NTYPE * N + SORTED_RING * 2 * WIN].rearrange(
            "p (q i n) -> p q i n", q=SORTED_RING, i=2)
        out_sb = h_sb
        fold = scratch[:, 0, 0:D]
        second_type = [(slice(0, P), 1, biased[:, 1, :]), (slice(WIN, P), 0, scratch[:, 0, D:2 * D])]

        psum = ctx.enter_context(nc.psum_tensor("psum", [P, 8, BANK], F32))
        pz = [psum[:, 2 * b:2 * b + 2, :].rearrange("p a n -> p (a n)") for b in range(2)]
        p_pair = [psum[:, 4 + c, :] for c in range(NT)]
        p_block = psum[:, 4:6, :].rearrange("p a n -> p (a n)")

        def psum2(b):
            return psum[:, b:b + 2, :].rearrange("p a n -> p (a n)")

        def z_tile(b, t):
            nodes = psum[:, b % 2, :].rearrange("p (k t n) -> p k t n", k=2, t=NT)[:, :, t, :]
            return nodes if t else nodes.rearrange("p k (q n) -> p k q n", q=2)

        p_bucketed = psum[:, 3, :]
        p_tr = [psum[:, 6 + b, :] for b in range(2)]

        x_in = [sem(f"x_in{t}") for t in range(NT)]
        ids_in = sem("ids_in")
        small_one = sem("small_one")
        small_in = sem("small_in")
        bias_in = sem("bias_in")
        w_in = [sem(f"w_in{i}") for i in range(RAW)]
        consts = sem("consts")
        dve_step = sem("dve_step")
        pool_step = sem("pool_step")
        ids_f = sem("ids_f")
        ids_T = sem("ids_T")
        ids_ready = sem("ids_ready")
        sum_ready = sem("sum_ready")
        sq_ready = sem("sq_ready")
        var_ready = sem("var_ready")
        std_ready = sem("std_ready")
        norm_ready = sem("norm_ready")
        h_ready = sem("h_ready")
        hT_done = sem("hT_done")
        hT_hi = sem("hT_hi")
        hT_lo = sem("hT_lo")
        hi_ready = sem("hi_ready")
        lo_ready = sem("lo_ready")
        lo_pool = sem("lo_pool")
        chunk_used = sem("chunk_used")
        tb_biased = sem("tb_biased")
        tb_hi = sem("tb_hi")
        tb_lo = sem("tb_lo")
        hot_ready = sem("hot_ready")
        tr_done = sem("tr_done")
        hotT_ready = sem("hotT_ready")
        gather_done = sem("gather_done")
        logit_ready = sem("logit_ready")
        shi_ready = sem("shi_ready")
        scaled_ready = sem("scaled_ready")
        scatter_done = sem("scatter_done")
        member_ready = sem("member_ready")
        ranks_done = sem("ranks_done")
        ranks_copied = sem("ranks_copied")
        running_ready = sem("running_ready")
        base_ready = sem("base_ready")
        places_ready = sem("places_ready")
        place_ready = sem("place_ready")
        lots_ready = sem("lots_ready")
        spread_ready = sem("spread_ready")
        spread_used = sem("spread_used")
        bucketed_ready = sem("bucketed_ready")
        route_ready = sem("route_ready")
        edgeT_done = sem("edgeT_done")
        edgeT_hi_ready = sem("edgeT_hi_ready")
        edgeT_ready = sem("edgeT_ready")
        biased_z = sem("biased_z")
        first_kept = sem("first_kept")
        first_complete = sem("first_complete")
        packed_ready = sem("packed_ready")
        folded = sem("folded")
        kept_folded = sem("kept_folded")
        summed_up = sem("summed_up")
        relu_done = sem("relu_done")
        second_ready = sem("second_ready")
        numbers_ready = sem("numbers_ready")
        pool_waited = sem("pool_waited")
        shot_ready = sem("shot_ready")
        blocks_ready = sem("blocks_ready")
        blocks_moved = sem("blocks_moved")
        pairs_ready = sem("pairs_ready")
        exp_bias = sem("exp_bias")
        exp_done = sem("exp_done")
        alpha_ready = sem("alpha_ready")
        alphaT_done = sem("alphaT_done")
        alphaT_ready = sem("alphaT_ready")
        z_done = sem("z_done")
        z_hi = sem("z_hi")
        z_lo = sem("z_lo")
        out_ready = sem("out_ready")
        out_saved = sem("out_saved")

        w_hh, w_oo, w_ho = w_edge
        w_hn, w_on = w_node
        halves = [(w_oo, 0), (w_oo, 1), (w_hh, 0), (w_hh, 1), (w_ho, 0), (w_hn, 0),
                  (w_ho, 1), (w_on, 0), (w_on, 1), (w_hn, 1)]
        OO, HH, HO_SRC, HN_H, HO_DST, ON_H, ON_Z, HN_Z = 0, 2, 4, 5, 6, 7, 8, 9

        table_slots = table[:, :, :, :, :].rearrange("p a t i d -> p (a t i) d")
        late_hi = [w_hi[:, (ON_H * KC + i) % SPLIT, :] for i in range(SPLIT)] + [table_slots[:, i, :] for i in range(4)]
        late_lo = [w_lo[:, (ON_H * KC + i) % SPLIT, :] for i in range(SPLIT)] + [table_slots[:, i + 4, :] for i in range(4)]
        LATE = len(late_hi)

        def row(v):
            return v.rearrange("(a d) -> a d", a=1).broadcast_to([P, v.shape[0]])

        def bc(a, shape, axis):
            v = a.rearrange("p (u n) -> p u n", u=1) if axis == 2 else a.rearrange("p (n u) -> p n u", u=1)
            return v.broadcast_to(shape)

        def wide(q):
            return hot[:, q, :, :]

        def slot_of(n):
            if n < ON_H * KC:
                return w_hi[:, n % SPLIT, :], w_lo[:, n % SPLIT, :]
            return late_hi[(n - ON_H * KC) % LATE], late_lo[(n - ON_H * KC) % LATE]

        def wait_slot(eng, n):
            if n < ON_H * KC + SPLIT:
                eng.wait_ge(chunk_used, n + 1 - SPLIT)
            elif n < ON_H * KC + LATE:
                eng.wait_ge(gather_done, all_tiles - 1)
            else:
                eng.wait_ge(chunk_used, n + 1 - LATE)

        def by_pool(n):
            s = n // KC
            return n % KC in {OO + 1: (4, 5, 6, 7), HH: (2, 4, 6), HH + 1: (0, 2, 4, 6), HN_H: (1, 3, 5), ON_H: range(KC),
                              ON_Z: (1, 3, 5, 7), HN_Z: (1, 3, 5, 6)}.get(s, ())

        def low_taken(n):
            if by_pool(n):
                return lo_pool, sum(by_pool(m) for m in range(n + 1))
            return lo_ready, sum(not by_pool(m) for m in range(n + 1))

        def tiles(eng, first, count, step):
            n = SORTED_RING
            rounds = count // n
            with eng.Fori(0, rounds) as r:
                for j in range(n):
                    step(r * n + (first + j), (first + j) % n)
            for t in range(first + rounds * n, first + count):
                step(t, t % n)

        block = ctx.enter_context(nc.Block())

        @block.sync
        def _(sp):
            sp.dma_start(x_sb[:, 0, :], x[0:P, :]).then_inc(x_in[0], 16)
            sp.dma_start(ids_rows_i[:, 0, :], src.rearrange("(t e) -> t e", e=P)).then_inc(ids_in, 16)
            sp.dma_start(ids_rows_i[:, 1, :], dst.rearrange("(t e) -> t e", e=P)).then_inc(ids_in, 16)
            sp.dma_start(x_sb[:, 1, :], x[P:N, :]).then_inc(x_in[1], 16)

            def half_matrix(w, half, s):
                for c in range(KC):
                    if s * KC + c >= RAW:
                        sp.wait_ge(*low_taken(s * KC + c - RAW))
                    sp.dma_start(w_raw[:, c % RAW, :], w[bass.ds(half * D + c * P, P), :]).then_inc(w_in[c % RAW], 16)

            for s, (w, half) in enumerate(halves):
                half_matrix(w, half, s)
            for t in range(NT):
                n = len(halves) * KC + t
                sp.wait_ge(*low_taken(n - RAW))
                sp.dma_start(w_raw[:, n % RAW, :], x[t * P:(t + 1) * P, :]).then_inc(w_in[n % RAW], 16)
            sp.wait_ge(second_ready, 1)
            sp.dma_start(out[P:N, :], out_sb[:, 1, :]).then_inc(out_saved, 16)
            sp.wait_ge(second_ready, 2)
            sp.dma_start(out[n_first:P, :], out_sb[n_first:P, 0, :]).then_inc(out_saved, 16)
            for h in range(HALVES):
                cols = slice(h * BANK, (h + 1) * BANK)
                sp.wait_ge(out_ready, 1 + h)
                sp.dma_start(out[0:n_first, cols], out_sb[0:n_first, 0, cols]).then_inc(out_saved, 16)
            sp.wait_ge(out_saved, 64)

        @block.gpsimd
        def _(pool):
            step = [0]

            def own(ins):
                step[0] += 1
                ins.then_inc(pool_step, 1)
                pool.wait_ge(pool_step, step[0])

            ts, tt = nc.gpsimd.tensor_scalar, nc.gpsimd.tensor_tensor
            own(nc.gpsimd.memset(ident[:, :], 0.0))
            nc.gpsimd.affine_select(out=ident[:, :], in_=ident[:, :], compare_op=ALU.not_equal, fill=1.0, base=0,
                                    pattern=[[-1, P]], channel_multiplier=1).then_inc(consts, 1)
            own(nc.gpsimd.iota(iota_i, pattern=[[1, N]], base=0, channel_multiplier=0))
            nc.gpsimd.tensor_copy(iota_row[:, :], iota_i).then_inc(consts, 1)
            pool.wait_ge(consts, 2)
            nc.gpsimd.tensor_copy(iota_half[:, :], iota_row[:, 0:P])
            nc.gpsimd.tensor_copy(ident_r[:, :], ident[:, :]).then_inc(consts, 1)
            nc.gpsimd.memset(zeros_r[:, :].bitcast(F32), 0.0).then_inc(consts, 1)
            nc.gpsimd.memset(ones[:, :], 1.0).then_inc(consts, 1)
            own(nc.gpsimd.memset(before[:, :], 1.0))
            own(nc.gpsimd.memset(upto_b, 1.0))
            nc.gpsimd.affine_select(out=upto_b, in_=upto_b, compare_op=ALU.is_ge, fill=0.0, base=0,
                                    pattern=[[1, NB], [-1, NB]], channel_multiplier=0).then_inc(consts, 1)
            nc.gpsimd.affine_select(out=before[:, :], in_=before[:, :], compare_op=ALU.is_gt, fill=0.0, base=0,
                                    pattern=[[1, P]], channel_multiplier=-1).then_inc(consts, 1)
            for i in range(2):
                own(ts(iota_win[:, i, :], iota_row[:, 0:WIN], 1.0, None, ALU.add))
            nc.gpsimd.dma_start(wa_row[:, :], row(w_a.rearrange("d a -> (d a)"))).then_inc(small_in, 16)
            nc.gpsimd.dma_start(ba_col[:, :], row(b_a)).then_inc(small_in, 16)
            nc.gpsimd.dma_start(bias[:, 1, :], row(b_node[0])).then_inc(small_in, 16)
            nc.gpsimd.dma_start(bias[:, 0, :], row(b_edge[1])).then_inc(small_in, 16)

            def whole(out_, tmp, in_, scale, shift):
                own(ts(tmp[0], in_, scale, shift, ALU.mult, ALU.add))
                own(ts(tmp[1], tmp[0], MAGIC, None, ALU.add))
                own(ts(out_, tmp[1], -MAGIC, None, ALU.add))

            def summed(out_, a):
                n = a.shape[1]
                while n > 2:
                    n //= 2
                    own(tt(a[:, 0:n, :], a[:, 0:n, :], a[:, n:2 * n, :], ALU.add))
                own(tt(out_, a[:, 0, :], a[:, 1, :], ALU.add))

            pool.wait_ge(ids_ready, 1)
            mine = ids[:, :, first_sorted:ET]
            window, number = ends[:, 0, :, :], ends[:, 1, :, :]
            whole(window, (ends_tmp[:, 0, :, :], ends_tmp[:, 1, :, :]), mine, 1.0 / WIN, 0.5 / WIN - 0.5)
            own(ts(ends_tmp[:, 2, :, :], window, -float(WIN), 1.0, ALU.mult, ALU.add))
            own(tt(number, ends_tmp[:, 2, :, :], mine, ALU.add))
            own(ts(bucket[:, 0, :], window[:, 1, :], float(NW), None, ALU.mult))
            own(tt(bucket[:, 1, :], bucket[:, 0, :], window[:, 0, :], ALU.add))

            def by_b(a):
                return a.rearrange("p (b t) -> p b t", b=NB)
            for b in range(NB):
                ins = ts(by_b(member)[:, b, :], bucket[:, 1, :], float(b), None, ALU.is_equal)
            ins.then_inc(member_ready, 1)
            pool.wait_ge(ranks_copied, 2)
            pool.wait_ge(running_ready, 1)
            run, tot = by_b(running), by_b(totals)
            end, count, tb_, upto, first_t, base = (by_bucket[:, i, :] for i in (0, 1, 4, 5, 6, 8))
            own(tt(end, run[:, :, CT - 1], tot[:, :, CT - 1], ALU.add))
            own(tt(count, end, run[:, :, 0], ALU.subtract))
            whole(tb_, (by_bucket[:, 2, :], by_bucket[:, 3, :]), count, 1.0 / P, 0.5 - 0.5 / P)
            S2 = [P, NB, NB]
            own(tt(upto_b, upto_b, bc(tb_, S2, 2), ALU.mult))
            summed(upto, upto_b.rearrange("p b c -> p c b"))
            own(tt(first_t, upto, tb_, ALU.subtract))
            own(ts(by_bucket[:, 7, :], first_t, float(P), None, ALU.mult))
            own(tt(base, by_bucket[:, 7, :], run[:, :, 0], ALU.subtract))
            pool.sem_inc(base_ready, 1)
            pool.wait_ge(places_ready, 1)
            pos, sorted_tile, slot = bucket[:, 2, :], bucket[:, 3, :], bucket[:, 4, :]
            summed(pos, by_b(place)[:, 0:NB // 2, :])
            whole(sorted_tile, (bucket_tmp[:, 0, :], bucket_tmp[:, 1, :]), pos, 1.0 / P, 0.5 / P - 0.5)
            own(ts(bucket_tmp[:, 2, :], sorted_tile, -float(P), None, ALU.mult))
            own(tt(slot, bucket_tmp[:, 2, :], pos, ALU.add))
            pool.sem_inc(place_ready, 1)

            def low_parts_by_pool(s):
                for n in filter(by_pool, range(s * KC, (s + 1) * KC)):
                    pool.wait_ge(hi_ready, n + 1)
                    tt(slot_of(n)[1], w_raw[:, n % RAW, :], slot_of(n)[0].bitcast(F32), ALU.subtract).then_inc(lo_pool, 1)
            low_parts_by_pool(OO + 1)
            rf = [route_f[:, i, :] for i in range(7)]
            for b in range(NB):
                ins = ts(route_b[:, b, :], iota_row[0:1, 0:ST], upto[0:1, b:b + 1], None, ALU.is_ge)
            own(ins)
            summed(rf[0], route_b)
            own(ts(rf[1], rf[0], float(NB - 1), None, ALU.min))
            for s in (HH, HH + 1):
                low_parts_by_pool(s)
            whole(rf[4], (rf[2], rf[3]), rf[1], 1.0 / NW, 0.5 / NW - 0.5)
            own(ts(rf[5], rf[4], -float(NW), None, ALU.mult))
            own(tt(rf[6], rf[5], rf[1], ALU.add))
            ts(rf[0], rf[6], float(D), None, ALU.mult)
            ts(rf[2], rf[4], float(D), float(NW * D), ALU.mult, ALU.add)
            own(ts(rf[3], rf[1], float(WIN), float(4 * BANK), ALU.mult, ALU.add))
            for i, offset in enumerate((rf[0], rf[2], rf[3])):
                ins = nc.gpsimd.tensor_copy(route[:, :, i], offset)
            ins.then_inc(route_ready, 1)
            pool.wait_ge(chunk_used, (HH + 2) * KC)
            for part, q in ((nfT_hi, slice(0, 4, 3)), (nfT_lo, slice(1, 3))):
                ins = nc.gpsimd.tensor_copy(packed[:, :, q, :],
                                            part[:, 0:KC, 0:P].rearrange("p k (q n) -> p k q n", q=2).bitcast(F32))
            ins.then_inc(packed_ready, 1)
            pool.wait_ge(bucketed_ready, 1)
            pool.wait_ge(scatter_done, first_sorted)

            def carried():
                pool.sem_inc(pool_waited, 1)

            def sorted_hots(r, n):
                if not (isinstance(r, int) and r == 0):
                    pool.wait_ge(shot_ready, r * SORTED_RING)
                    carried()
                nc.gpsimd.tensor_copy(numbers[:, 0:n, :], bucketed[:, :, bass.ds(r * SORTED_RING, n)]
                                      .rearrange("p a t -> p t a")).then_inc(numbers_ready, 1)
                pool.wait_ge(numbers_ready, r + 1)
                carried()
                for j in range(n):
                    if j % 2 == 0 and not (isinstance(r, int) and r == 0):
                        pool.wait_ge(scatter_done, r * SORTED_RING + (first_sorted + min(j + 2, n) - SORTED_RING))
                        carried()
                    for a, part in enumerate((DST, SRC)):
                        ins = ts(sorted_hot[:, (first_sorted + j) % SORTED_RING, part:part + 2, :], iota_win[:, :, :],
                                 numbers[:, j, a:a + 1], None, ALU.is_equal)
                    ins.then_inc(shot_ready, 1)
            sorted_hots(0, SORTED_RING)
            low_parts_by_pool(HN_H)
            with pool.Fori(1, ST // SORTED_RING) as r:
                sorted_hots(r, SORTED_RING)
            if ST % SORTED_RING:
                sorted_hots(ST // SORTED_RING, ST % SORTED_RING)
            low_parts_by_pool(ON_H)
            low_parts_by_pool(ON_Z)
            low_parts_by_pool(HN_Z)
            for i, (rows, t, sums) in enumerate(second_type):
                n = len(halves) * KC + t
                pool.wait_ge(w_in[n % RAW], 16 * (n // RAW + 1))
                pool.wait_ge(relu_done, i + 1)
                if i:
                    pool.wait_ge(second_ready, i)
                tt(out_sb[rows, t, :], sums[rows, :], w_raw[rows, n % RAW, :], ALU.add).then_inc(second_ready, 1)

        @block.scalar
        def _(act):
            act.wait_ge(small_one, 1)
            nc.scalar.activation(small[:, 6, 0:1], small[:, 7, 0:1], ACT.Sqrt)
            for t in range(NT):
                act.wait_ge(sum_ready, t + 1)
                nc.scalar.activation(biased[:, t, :], x_sb[:, t, :], ACT.Square, bias=stats[:, 1, t:t + 1],
                                     accum_out=stats[:, 2, t:t + 1]).then_inc(sq_ready, 1)
                act.wait_ge(var_ready, t + 1)
                nc.scalar.activation(stats[:, 4, t:t + 1], stats[:, 3, t:t + 1], ACT.Sqrt).then_inc(std_ready, 1)
            for t in range(NT):
                act.wait_ge(norm_ready, t + 1)
                nc.scalar.activation(h_sb[:, t, :], x_sb[:, t, :], ACT.Relu, bias=stats[:, 9, t:t + 1],
                                     scale=stats[:, 8, t:t + 1]).then_inc(h_ready, 1)

            def split4(dst_, done, ready, first_bank, banks=range(4)):
                for k in banks:
                    act.wait_ge(done, k + 1)
                    nc.scalar.copy(dst_[:, k, :], psum[:, first_bank + k, :]).then_inc(ready, 1)

            def high_parts(s, between={}, first=0, upto=KC):
                for c in range(first, upto):
                    n = s * KC + c
                    act.wait_ge(w_in[n % RAW], 16 * (n // RAW + 1))
                    if n >= SPLIT:
                        wait_slot(act, n)
                    nc.scalar.copy(slot_of(n)[0], w_raw[:, n % RAW, :]).then_inc(hi_ready, 1)
                    if c in between:
                        between[c]()

            def ranks_out():
                act.wait_ge(ranks_done, 1)
                for a, b in ((earlier, 4), (totals, 6)):
                    nc.scalar.copy(a.rearrange("p (i n) -> p i n", i=2),
                                   psum[:, b:b + 2, 0:BC // 2]).then_inc(ranks_copied, 1)

            def table_hi(i, end, t):
                if end:
                    act.wait_ge(chunk_used, (OO + 2) * KC)
                else:
                    act.wait_ge(tb_biased, t + 1)
                from_ = psum2(4 + 2 * t) if end else biased[:, t, :]
                nc.scalar.copy(table[:, end, t, 0, :], from_).then_inc(tb_hi, 1)

            def win_table_hi(i, end, t, j):
                if end:
                    act.wait_ge(*((chunk_used, (HO_DST + 1) * KC) if t else (first_complete, 1)))
                else:
                    act.wait_ge(tb_biased, NT + t + 1)
                act.wait_ge(gather_done, first_sorted - 1)
                rows = slice(j * WIN, (j + 1) * WIN)
                from_ = psum2(2 * t) if end else biased[:, t, :]
                nc.scalar.copy(win_table[rows, end, 2 * t + j, :], from_[rows, :]).then_inc(tb_hi, 1)

            def load_bias(b):
                act.dma_start(bias[:, 0, :], row(b)).then_inc(bias_in, 16)

            def pairs_out(m, upto):
                act.wait_ge(scatter_done, upto)
                for c in range(NT):
                    nc.scalar.copy(pairs[:, c, m, :, :].rearrange("p a n -> p (a n)"), p_pair[c]).then_inc(pairs_ready, 1)

            def transposed(t, b, parts=4, bank=None):
                act.wait_ge(tr_done, t + 1)
                if not isinstance(t, int) or t > 2:
                    act.wait_ge(gather_done, t - 2)
                elif t == 2:
                    act.wait_ge(edgeT_done, 4)
                nc.scalar.copy(hotT[:, b, 0:parts, :].rearrange("p c e -> p (c e)"),
                               (bank or p_tr[b])[:, 0:parts * P]).then_inc(hotT_ready, 1)

            h_hi = nfT_hi[:, 0:KC, :].rearrange("p (k a) n -> p k (a n)", a=2)
            high_parts(OO, upto=1)
            split4(h_hi, hT_done, hT_hi, 4, range(1))
            high_parts(OO, first=1, upto=2)
            split4(h_hi, hT_done, hT_hi, 4, range(1, 4))
            high_parts(OO, {3: ranks_out}, first=2)
            high_parts(OO + 1, {1: lambda: table_hi(0, 0, 0), 2: lambda: table_hi(0, 0, 1),
                                5: lambda: transposed(0, 0, 4, pz[0])})
            split4(edgeT_hi.rearrange("p (k a) e -> p k (a e)", a=4), edgeT_done, edgeT_hi_ready, 0)
            high_parts(HH, {1: lambda: table_hi(1, 1, 0), 2: lambda: table_hi(1, 1, 1), 3: lambda: load_bias(b_edge[0])})
            high_parts(HH + 1)
            act.wait_ge(spread_used, CT // GROUP)
            nc.scalar.copy(bucketed[:, :, :].rearrange("p a t -> p (a t)"),
                           p_bucketed[:, 0:2 * ST]).then_inc(bucketed_ready, 1)
            for t in range(1, first_sorted):
                transposed(t, t % 2)
                if t == 3:
                    act.wait_ge(route_ready, 1)
                    pairs_out(0, 1)
                    load_bias(b_edge[2])
            high_parts(HO_SRC, upto=SPLIT)
            pairs_out(1, first_sorted)
            high_parts(HO_SRC, first=SPLIT)
            high_parts(HN_H)

            def keep_low_rows():
                act.wait_ge(tb_lo, 8)
                act.wait_ge(chunk_used, (HN_H + 1) * KC)
                nc.scalar.copy(biased[0:WIN, 1, :], psum2(4)[WIN:P, :]).then_inc(first_kept, 1)
            table_parts = {1 + 2 * t + j: (lambda t=t, j=j: win_table_hi(2, 0, t, j)) for t in range(NT) for j in range(2)}
            high_parts(HO_DST, table_parts | {6: keep_low_rows})
            for t in range(NT):
                for j in range(2):
                    win_table_hi(3, 1, t, j)
            load_bias(b_node[1])

            def scaled(t, q):
                nc.scalar.copy(added[:, q, 1, :], sorted_hot[:, q, DST, :].bitcast(F32))
                act.wait_ge(logit_ready, t + 1)
                nc.scalar.activation(added[:, q, 0, :], sorted_hot[:, q, DST, :].bitcast(F32), ACT.Copy,
                                     scale=logit[:, q:q + 1]).then_inc(scaled_ready, 1)

            def sorted_step(t, q):
                transposed(t + 1, (q + 1) % 2, 2)
                scaled(t - 1, (q - 1) % SORTED_RING)
            f, last = first_sorted, all_tiles - 1
            transposed(f, f % 2, 2)
            transposed(f + 1, (f + 1) % 2, 2)
            straight = f + 1 + (last - f - 1) // SORTED_RING * SORTED_RING - SORTED_RING
            tiles(act, f + 1, straight - f - 1, sorted_step)
            for t in range(straight, last):
                sorted_step(t, t % SORTED_RING)
                c, odd = divmod(t - straight, 2)
                if odd and c < SPLIT:
                    high_parts(ON_H, first=c, upto=c + 1)
            scaled(last - 1, (last - 1) % SORTED_RING)
            scaled(last, last % SORTED_RING)
            act.wait_ge(scatter_done, all_tiles)
            nc.scalar.copy(blocks, p_block).then_inc(blocks_ready, 1)
            act.wait_ge(blocks_ready, 1)
            for j in range(2):
                for a in range(2):
                    act.dma_start(pairs[j * WIN:(j + 1) * WIN, :, 2, a, :],
                                  blocks[a * WIN:(a + 1) * WIN, :].rearrange("p (c j n) -> p j c n", c=NT, j=2)[:, j, :, :]
                                  ).then_inc(blocks_moved, 16)
            high_parts(ON_H, first=SPLIT)
            for c in range(NT):
                act.wait_ge(exp_bias, 1)
                nc.scalar.activation(shifted[:, c, :], shifted[:, c, :], ACT.Exp,
                                     bias=small[:, 1, c:c + 1]).then_inc(exp_done, 1)
            high_parts(ON_Z, upto=5)
            act.wait_ge(alphaT_done, 1)
            nc.scalar.copy(alphaT.rearrange("p c n -> p (c n)"), psum[:, 0, :]).then_inc(alphaT_ready, 1)
            for k in range(4):
                act.wait_ge(z_done, k + 1)
                two = slice(2 * k, 2 * k + 2)
                nc.scalar.copy(packed[:, two, 0:4:3, :], z_tile(k, 0)).then_inc(z_hi, 1)
                nc.scalar.copy(z1[:, two, 0, :], z_tile(k, 1)).then_inc(z_hi, 1)
                if k:
                    high_parts(ON_Z, first=4 + k, upto=5 + k)
            high_parts(HN_Z)

            def fold_out(complete, bank, rows, cols):
                own_rows = slice(WIN - rows.start, P - rows.start)
                act.wait_ge(*complete)
                nc.scalar.copy(fold[own_rows, cols], psum2(bank)[rows, cols]).then_inc(folded, 1)
            fold_out((chunk_used, (ON_Z + 1) * KC), 4, slice(0, WIN), slice(0, D))

            def second_relu(i):
                rows, _, sums = second_type[i]
                act.wait_ge(summed_up, i + 1)
                nc.scalar.activation(sums[rows, :], sums[rows, :], ACT.Relu).then_inc(relu_done, 1)
            second_relu(0)
            fold_out((first_complete, 2), 2, slice(WIN, P), slice(0, BANK))
            fold_out((chunk_used, (HN_Z + 1) * KC), 2, slice(WIN, P), slice(BANK, D))
            second_relu(1)

        @block.vector
        def _(dve):
            step = [0]

            def own(ins):
                step[0] += 1
                ins.then_inc(dve_step, 1)
                dve.wait_ge(dve_step, step[0])

            nc.vector.memset(small[:, 7, 0:1], 1.0).then_inc(small_one, 1)
            for t in range(NT):
                dve.wait_ge(x_in[t], 16)
                own(nc.vector.tensor_reduce(stats[:, 0, t:t + 1], x_sb[:, t, :], AX.X, ALU.add))
                nc.vector.tensor_scalar(stats[:, 1, t:t + 1], stats[:, 0, t:t + 1], -1.0 / D, None,
                                        ALU.mult).then_inc(sum_ready, 1)
                if t == 0:
                    dve.wait_ge(ids_in, 32)
                    nc.vector.tensor_copy(ids_rows, ids_rows_i).then_inc(ids_f, 1)

            def variance(t):
                dve.wait_ge(sq_ready, t + 1)
                nc.vector.tensor_scalar(stats[:, 3, t:t + 1], stats[:, 2, t:t + 1], 1.0 / D, EPS, ALU.mult,
                                        ALU.add).then_inc(var_ready, 1)
            dve.wait_ge(ids_T, 1)
            nc.vector.tensor_copy(ids[:, :, :],
                                  p_tr[0][:, 0:2 * ET].rearrange("p (a t) -> p a t", a=2)).then_inc(ids_ready, 1)
            for t in range(NT):
                row_ = [stats[:, i, t:t + 1] for i in range(10)]
                if t == 0:
                    variance(0)
                dve.wait_ge(std_ready, t + 1)
                own(nc.vector.reciprocal(row_[5], row_[4]))
                own(nc.vector.tensor_tensor(row_[6], row_[5], row_[5], ALU.mult))
                own(nc.vector.tensor_tensor(row_[7], row_[6], row_[3], ALU.mult))
                own(nc.vector.tensor_scalar(row_[6], row_[7], -0.5, 1.5, ALU.mult, ALU.add))
                own(nc.vector.tensor_tensor(row_[8], row_[5], row_[6], ALU.mult))
                nc.vector.tensor_tensor(row_[9], row_[8], row_[1], ALU.mult).then_inc(norm_ready, 1)
                if t == 0:
                    variance(1)

            def split4(dst_lo, dst_hi, hi, ready, first_bank):
                for k in range(4):
                    dve.wait_ge(hi, k + 1)
                    nc.vector.tensor_tensor(dst_lo[:, k, :], psum[:, first_bank + k, :], dst_hi[:, k, :].bitcast(F32),
                                            ALU.subtract).then_inc(ready, 1)

            def low_parts(s, between={}, first=0, upto=KC):
                for c in range(first, upto):
                    n = s * KC + c
                    if not by_pool(n):
                        dve.wait_ge(hi_ready, n + 1)
                        nc.vector.tensor_tensor(slot_of(n)[1], w_raw[:, n % RAW, :], slot_of(n)[0].bitcast(F32),
                                                ALU.subtract).then_inc(lo_ready, 1)
                    if c in between:
                        between[c]()

            def one_hots(t, q):
                if t >= RING:
                    dve.wait_ge(scatter_done, t + (1 - RING))
                for end in range(2):
                    ins = nc.vector.tensor_scalar(wide(q)[:, 2 + end, :], iota_row[:, :], ids[:, end, t:t + 1], None,
                                                  ALU.is_equal)
                ins.then_inc(hot_ready, 1)

            def weighted_sum(z, q):
                nc.vector.scalar_tensor_tensor(out=z, in0=z, scalar=0.0, in1=wa_row[:, :], op0=ALU.max,
                                               op1=ALU.mult, accum_out=logit[:, q:q + 1]).then_inc(logit_ready, 1)

            def scaled(t, q):
                dve.wait_ge(logit_ready, t + 1)
                nc.vector.tensor_scalar(wide(q)[:, 1, :], wide(q)[:, 2, :].bitcast(F32), logit[:, q:q + 1], None,
                                        ALU.mult).then_inc(shi_ready, 1)
                dve.wait_ge(shi_ready, t + 1)
                nc.vector.scalar_tensor_tensor(out=wide(q)[:, 0, :], in0=wide(q)[:, 2, :].bitcast(F32),
                                               scalar=logit[:, q:q + 1], in1=wide(q)[:, 1, :].bitcast(F32),
                                               op0=ALU.mult, op1=ALU.subtract).then_inc(scaled_ready, 1)

            def with_bias(k, s, t, loads=0):
                if t == 0:
                    dve.wait_ge(*((bias_in, 16 * loads) if loads else (small_in, 64)))
                dve.wait_ge(chunk_used, (s + 1) * KC)
                if k:
                    dve.wait_ge(tb_hi, NT)
                nc.vector.tensor_tensor(biased[:, t, :], psum2(2 * t), bias[:, 0, :], ALU.add).then_inc(tb_biased, 1)

            def table_lo(i, end, t):
                dve.wait_ge(tb_hi, NT * i + t + 1)
                nc.vector.tensor_tensor(table[:, end, t, 1, :], psum2(4 + 2 * t) if end else biased[:, t, :],
                                        table[:, end, t, 0, :].bitcast(F32), ALU.subtract).then_inc(tb_lo, 1)

            def win_table_lo(i, end, t, j):
                dve.wait_ge(tb_hi, 4 * (i - 1) + 2 * t + j + 1)
                rows, other = slice(j * WIN, (j + 1) * WIN), slice((1 - j) * WIN, (2 - j) * WIN)
                from_ = psum2(2 * t) if end else biased[:, t, :]
                nc.vector.tensor_tensor(win_table[other, end, 2 * t + j, :], from_[rows, :],
                                        win_table[rows, end, 2 * t + j, :].bitcast(F32),
                                        ALU.subtract).then_inc(tb_lo, 1)

            def running_sums():
                dve.wait_ge(ranks_copied, 2)
                own(nc.vector.tensor_tensor_scan(running, totals, totals, 0.0, ALU.add, ALU.bypass))
                nc.vector.tensor_tensor(running, running, totals, ALU.subtract).then_inc(running_ready, 1)

            def places():
                S3 = [P, NB, CT]
                place_b = place.rearrange("p (b t) -> p b t", b=NB)
                dve.wait_ge(base_ready, 1)
                own(nc.vector.tensor_tensor(place, earlier, running, ALU.add))
                own(nc.vector.tensor_tensor(place_b, place_b, bc(by_bucket[:, 8, :], S3, 1), ALU.add))
                own(nc.vector.tensor_tensor(place, place, member, ALU.mult))
                nc.vector.tensor_tensor(place[:, 0:BC // 2], place[:, 0:BC // 2], place[:, BC // 2:BC],
                                        ALU.add).then_inc(places_ready, 1)

            def lots_group(g):
                def slots():
                    if g == 0:
                        dve.wait_ge(place_ready, 1)
                    if g >= 2:
                        dve.wait_ge(spread_used, g - 1)
                    for t in range(GROUP):
                        col = slice(g * GROUP + t, g * GROUP + t + 1)
                        ins = nc.vector.tensor_scalar(spread[g % 2][:, t, :], iota_half[:, :], bucket[:, 4, col], None,
                                                      ALU.is_equal)
                    ins.then_inc(spread_ready, 1)

                group = slice(g * GROUP, (g + 1) * GROUP)
                S = [P, GROUP, ST]
                dst_lots, src_lots = lots[g % 2][:, :, 0, :], lots[g % 2][:, :, 1, :]

                def in_tile():
                    own(nc.vector.tensor_tensor(dst_lots, bc(iota_row[:, 0:ST], S, 2), bc(bucket[:, 3, group], S, 1),
                                                ALU.is_equal))

                def lot_numbers():
                    nc.vector.tensor_tensor(src_lots, dst_lots, bc(ends[:, 1, 0, group], S, 1), ALU.mult)
                    nc.vector.tensor_tensor(dst_lots, dst_lots, bc(ends[:, 1, 1, group], S, 1),
                                            ALU.mult).then_inc(lots_ready, 1)
                return slots, in_tile, lot_numbers

            total = pairs[:, :, :, 0, :]
            count_ = pairs[:, :, :, 1, :]
            means = shifted.rearrange("p c (m n) -> p c m n", m=NTYPE)

            def mean_steps(c, m, i):
                size = (c.stop - c.start) * N
                work = [scratch[:, 1, i * NTYPE * N + j * size:i * NTYPE * N + (j + 1) * size]
                        .rearrange("p (c n) -> p c n", n=N) for j in range(3)]
                tot, cnt, res = total[:, c, m, :], count_[:, c, m, :], means[:, c, m, :]
                return [lambda: own(nc.vector.tensor_scalar(work[0], cnt, 1.0, None, ALU.max)),
                        lambda: own(nc.vector.reciprocal(work[1], work[0])),
                        lambda: own(nc.vector.tensor_tensor(work[2], tot, work[1], ALU.mult)),
                        lambda: own(nc.vector.tensor_scalar(work[0], cnt, 0.0, ABSENT, ALU.is_equal, ALU.mult)),
                        lambda: own(nc.vector.scalar_tensor_tensor(out=res, in0=work[2], scalar=ba_col[:, 0:1],
                                                                   in1=work[0], op0=ALU.add, op1=ALU.add))]
            early = []
            for i, (m, c) in enumerate((m, c) for m in range(2) for c in range(NT)):
                steps = mean_steps(slice(c, c + 1), m, i % 3)
                early += [lambda m=m, a=steps: (dve.wait_ge(pairs_ready, (m + 1) * NT), a[0](), a[1]()),
                          lambda a=steps: (a[2](), a[3](), a[4]())]

            dve.wait_ge(consts, 2)
            group_lots = [lots_group(g) for g in range(CT // GROUP)]
            low_parts(OO, upto=1)
            split4(nfT_lo[:, 0:KC, :].rearrange("p (k a) n -> p k (a n)", a=2),
                   nfT_hi[:, 0:KC, :].rearrange("p (k a) n -> p k (a n)", a=2), hT_hi, hT_lo, 4)
            low_parts(OO, {2: lambda: one_hots(0, 0), 3: running_sums, 7: places}, first=1)
            low_parts(OO + 1, {0: lambda: with_bias(0, OO, 0), 1: lambda: with_bias(0, OO, 1),
                               2: lambda: table_lo(0, 0, 0), 3: lambda: table_lo(0, 0, 1),
                               4: lambda: (group_lots[0][0](), group_lots[0][1](), group_lots[0][2](), group_lots[1][0]()),
                               7: lambda: (group_lots[1][1](), group_lots[1][2]())})
            split4(edgeT_lo.rearrange("p (k a) e -> p k (a e)", a=4), edgeT_hi.rearrange("p (k a) e -> p k (a e)", a=4),
                   edgeT_hi_ready, edgeT_ready, 0)
            low_parts(HH, {1: lambda: table_lo(1, 1, 0), 2: lambda: table_lo(1, 1, 1),
                           3: group_lots[2][0], 5: group_lots[2][1], 6: group_lots[2][2], 7: group_lots[3][0]})
            low_parts(HH + 1, {1: group_lots[3][1], 3: group_lots[3][2]})
            one_hots(1, 1)
            one_hots(2, 2)
            dve.wait_ge(bias_in, 16)
            dve.wait_ge(chunk_used, (HH + 2) * KC)
            nc.vector.tensor_tensor(biased[:, 1, :], pz[0], bias[:, 0, :], ALU.add).then_inc(biased_z, 1)
            dve.wait_ge(biased_z, 1)
            weighted_sum(biased[:, 1, :], 0)
            scaled(0, 0)
            one_hots(3, 3)
            for t in range(1, first_sorted):
                if RING <= t + 2 < first_sorted:
                    one_hots(t + 2, (t + 2) % RING)
                dve.wait_ge(gather_done, t)
                weighted_sum(pz[t % 2], t % RING)
                scaled(t, t % RING)
                if t >= 3:
                    low_parts(HO_SRC, first=t - 3, upto=t - 2)
                if t == 4:
                    early[0]()
            low_parts(HO_SRC, {c: early[c + 1 - SPLIT] for c in range(SPLIT, KC)}, first=SPLIT)
            low_parts(HN_H, {0: lambda: with_bias(1, HO_SRC, 0, 2), 2: lambda: with_bias(1, HO_SRC, 1, 2)})
            first_rows = slice(0, WIN)

            def keep_high_rows():
                dve.wait_ge(tb_hi, 8)
                dve.wait_ge(chunk_used, (HN_H + 1) * KC)
                nc.vector.tensor_tensor(biased[first_rows, 0, :], psum2(4)[first_rows, :], bias[first_rows, 1, :],
                                        ALU.add).then_inc(first_kept, 1)
            between = {1 + 2 * t + j: (lambda t=t, j=j: win_table_lo(2, 0, t, j)) for t in range(NT) for j in range(2)}
            low_parts(HO_DST, between | {0: early[6], 5: early[7], 7: keep_high_rows})
            for t in range(NT):
                for j in range(2):
                    win_table_lo(3, 1, t, j)

            def sorted_logit(t, q):
                dve.wait_ge(gather_done, t)
                weighted_sum(pz[q % 2], q)
            tiles(dve, first_sorted, ST, sorted_logit)

            nc.vector.tensor_tensor(biased[first_rows, 0, :], biased[first_rows, 0, :], biased[first_rows, 1, :],
                                    ALU.add).then_inc(kept_folded, 1)
            dve.wait_ge(blocks_moved, 64)
            for step_ in mean_steps(slice(0, NT), 2, 0):
                step_()
            own(nc.vector.tensor_reduce(small[:, 0, :], shifted, AX.X, ALU.max))
            nc.vector.tensor_scalar(small[:, 1, :], small[:, 0, :], -1.0, None, ALU.mult).then_inc(exp_bias, 1)
            for c in range(NT):
                dve.wait_ge(exp_done, c + 1)
                weights = soft[:, c, 0:NTYPE * N].rearrange("p (m n) -> p m n", m=NTYPE)
                own(nc.vector.scalar_tensor_tensor(out=weights, in0=means[:, c, :, :], scalar=1.0,
                                                   in1=count_[:, c, :, :], op0=ALU.mult, op1=ALU.mult,
                                                   accum_out=small[:, 2, c:c + 1]))
                own(nc.vector.tensor_scalar(small[:, 3, c:c + 1], small[:, 2, c:c + 1], 0.5, None, ALU.max))
                own(nc.vector.reciprocal(small[:, 4, c:c + 1], small[:, 3, c:c + 1]))
                own(nc.vector.tensor_tensor(soft[:, 2, 0:N], weights[:, 0, :], weights[:, 1, :], ALU.add))
                own(nc.vector.tensor_tensor(soft[:, 2, N:2 * N], soft[:, 2, 0:N], weights[:, 2, :], ALU.add))
                nc.vector.tensor_scalar(alpha[:, c, :], soft[:, 2, N:2 * N], small[:, 4, c:c + 1], None,
                                        ALU.mult).then_inc(alpha_ready, 1)
            low_parts(ON_Z, upto=3)
            for k in range(4):
                if k >= 2:
                    low_parts(ON_Z, first=2 * k, upto=2 * k + 2)
                dve.wait_ge(z_hi, 2 * (k + 1))
                two = slice(2 * k, 2 * k + 2)
                nc.vector.tensor_tensor(packed[:, two, 1:3, :], z_tile(k, 0), packed[:, two, 0:4:3, :].bitcast(F32),
                                        ALU.subtract)
                nc.vector.tensor_tensor(z1[:, two, 1, :], z_tile(k, 1), z1[:, two, 0, :].bitcast(F32),
                                        ALU.subtract).then_inc(z_lo, 1)
            low_parts(HN_Z)

            dve.wait_ge(bias_in, 48)
            dve.wait_ge(kept_folded, 1)
            dve.wait_ge(chunk_used, (ON_Z + 1) * KC)
            for rows, t, sums in second_type:
                ins = nc.vector.tensor_tensor(sums[rows, :], psum2(4 + 2 * t)[rows, :], bias[rows, 0, :], ALU.add)
                if t == 0:
                    own(ins)
                    dve.wait_ge(folded, 1)
                    ins = nc.vector.tensor_tensor(sums[rows, :], sums[rows, :], fold[rows, :], ALU.add)
                ins.then_inc(summed_up, 1)
            n = len(halves) * KC
            dve.wait_ge(w_in[n % RAW], 16 * (n // RAW + 1))
            kept = biased[first_rows, 0, :]
            for h, complete in enumerate(((first_complete, 2), (chunk_used, (HN_Z + 1) * KC))):
                cols = slice(h * BANK, (h + 1) * BANK)
                dve.wait_ge(*complete)
                own(nc.vector.tensor_tensor(kept[:, cols], psum2(2)[first_rows, cols], kept[:, cols], ALU.add))
                dve.wait_ge(folded, 2 + h)
                own(nc.vector.tensor_tensor(kept[:, cols], kept[:, cols], fold[first_rows, cols], ALU.add))
                nc.vector.scalar_tensor_tensor(out=out_sb[first_rows, 0, cols], in0=kept[:, cols], scalar=0.0,
                                               in1=w_raw[first_rows, n % RAW, cols], op0=ALU.max,
                                               op1=ALU.add).then_inc(out_ready, 1)

        @block.tensor
        def _(pe):
            pe.wait_ge(ids_f, 1)
            pe.wait_ge(consts, 7)
            for end in range(2):
                ins = nc.tensor.transpose(p_tr[0][:, end * ET:(end + 1) * ET], ids_rows[:, end, :], ident[0:ET, 0:ET])
            ins.then_inc(ids_T, 1)
            pe.wait_ge(ids_ready, 1)
            for t in range(NT):
                pe.wait_ge(h_ready, t + 1)
                for k in range(KC):
                    ins = nc.tensor.transpose(psum[:, 4 + k // 2, k % 2 * N + t * P:k % 2 * N + (t + 1) * P],
                                              h_sb[:, t, k * P:(k + 1) * P], ident[:, :])
                    if t == NT - 1 and k % 2:
                        ins.then_inc(hT_done, 1)

            def product(s, outs, opens, closes, between={}, open_after={}, apart=0):
                def add(c, bank, passes, bank_halves=range(HALVES)):
                    steps = passes(c)
                    if c == 0 and bank in open_after:
                        pe.wait_ge(*open_after[bank])
                    for n, (left, w_low) in enumerate(steps):
                        for h in bank_halves:
                            ins = nc.tensor.matmul(psum[:, bank + h, :], left,
                                                   slot_of(s * KC + c)[w_low][:, h * BANK:(h + 1) * BANK],
                                                   start=(opens and c == 0 and n == 0),
                                                   stop=(closes and c == KC - 1 and n == len(steps) - 1))
                    return ins

                for c in range(KC - apart):
                    pe.wait_ge(*low_taken(s * KC + c))
                    for out_ in outs:
                        ins = add(c, *out_)
                    ins.then_inc(chunk_used, 1)
                    if c in between:
                        between[c]()
                for i, out_ in enumerate(outs if apart else []):
                    for c in range(KC - apart, KC):
                        if i == 0:
                            pe.wait_ge(*low_taken(s * KC + c))
                        ins = add(c, *out_)
                        if i == len(outs) - 1:
                            ins.then_inc(chunk_used, 1)
                    if i == 0:
                        ins.then_inc(first_complete, 1)

            def split_rows(hi, lo):
                return lambda c: [(hi(c), 0), (hi(c), 1), (lo(c), 0)]

            def h_rows(t):
                cols = slice(t * P, (t + 1) * P)
                return split_rows(lambda c: nfT_hi[:, c, cols], lambda c: nfT_lo[:, c, cols])

            def packed_rows(j):
                return lambda c: [(packed[:, c, 2 * j:2 * j + 2, :].rearrange("p q n -> p (q n)"), w_low)
                                  for w_low in range(2)]

            def products_of(s, end, between={}, open_after={}, apart=0):
                product(s, [(4 * end + 2 * t, h_rows(t)) for t in range(NT)], True, True, between, open_after, apart)

            def ranks():
                pe.wait_ge(hT_lo, 4)
                pe.wait_ge(member_ready, 1)
                for b, m in ((4, before), (6, ones)):
                    for h in range(2):
                        ins = nc.tensor.matmul(psum[:, b + h, 0:BC // 2], m[:, :], member[:, h * BC // 2:(h + 1) * BC // 2],
                                               start=True, stop=True)
                ins.then_inc(ranks_done, 1)

            def spread_group(g):
                pe.wait_ge(spread_ready, g + 1)
                pe.wait_ge(lots_ready, g + 1)
                for t in range(GROUP):
                    ins = nc.tensor.matmul(p_bucketed[:, 0:2 * ST], spread[g % 2][:, t, :],
                                           lots[g % 2][:, t, :, :].rearrange("p a s -> p (a s)"),
                                           start=(g == 0 and t == 0), stop=(g == CT // GROUP - 1 and t == GROUP - 1),
                                           skip_group_check=True)
                ins.then_inc(spread_used, 1)

            def open_pairs():
                for c in range(NT):
                    for i in range(BANK // P):
                        nc.tensor.matmul(p_pair[c][:, i * P:(i + 1) * P], zeros_r[:, :], zeros_r[:, :],
                                         start=(i == 0), stop=False, skip_group_check=True)

            def transposes(t, q, bank=None):
                b = q % 2
                pe.wait_ge(hot_ready, t + 1)
                if t >= 2:
                    pe.wait_ge(hotT_ready, t - 1)
                for end in range(2):
                    for c in range(NT):
                        j = 2 * end + c
                        ins = nc.tensor.transpose((bank or p_tr[b])[:, j * P:(j + 1) * P].bitcast(F32R),
                                                  wide(q)[:, 2 + end, c * P:(c + 1) * P], ident_r[:, :])
                ins.then_inc(tr_done, 1)

            def gather(t, q):
                b = q % 2
                pe.wait_ge(hotT_ready, t + 1)
                if t >= 2:
                    pe.wait_ge(logit_ready, t - 1)
                n = 0
                for end in range(2):
                    for c in range(NT):
                        for part in range(2):
                            for h in range(HALVES):
                                ins = nc.tensor.matmul(pz[b][:, h * BANK:(h + 1) * BANK], hotT[:, b, 2 * end + c, :],
                                                       table[:, end, c, part, h * BANK:(h + 1) * BANK],
                                                       start=(n == 0), stop=(n == 7))
                            n += 1
                ins.then_inc(gather_done, 1)

            def scatter(t, q):
                pe.wait_ge(scaled_ready, t + 1)
                for c in range(NT):
                    lhs = wide(q)[:, 3, c * P:(c + 1) * P]
                    nc.tensor.matmul(p_pair[c], lhs, wide(q)[:, 1:3, :].rearrange("p a n -> p (a n)"),
                                     start=False, stop=False, skip_group_check=True)
                    ins = nc.tensor.matmul(p_pair[c][:, 0:N], lhs, wide(q)[:, 0, :],
                                           start=False, stop=False, skip_group_check=True)
                ins.then_inc(scatter_done, 1)

            def first_transposes():
                pe.wait_ge(tb_biased, NT)
                transposes(0, 0, pz[0])

            def edge_features():
                pe.wait_ge(hotT_ready, 1)
                for j in range(2 * KC):
                    end, k = j // KC, j % KC
                    for t in range(NT):
                        ins = nc.tensor.matmul(psum[:, j // 4, (j % 4) * P:(j % 4 + 1) * P],
                                               h_sb[:, t, k * P:(k + 1) * P], hotT[:, 0, 2 * end + t, :].bitcast(F32),
                                               start=(t == 0), stop=(t == NT - 1))
                    if j % 4 == 3:
                        ins.then_inc(edgeT_done, 1)

            pe.wait_ge(hT_lo, 1)
            products_of(OO, 0, {1: ranks})
            pe.wait_ge(ranks_copied, 2)
            products_of(OO + 1, 1, {3: first_transposes, 5: edge_features})
            pe.wait_ge(edgeT_ready, 4)
            edges = [[(0, split_rows(lambda c, o=o: edgeT_hi[:, o + c, :], lambda c, o=o: edgeT_lo[:, o + c, :]))]
                     for o in (0, KC)]
            product(HH, edges[0], True, False, {1: lambda: spread_group(0), 3: lambda: spread_group(1)})
            product(HH + 1, edges[1], False, True, {1: lambda: spread_group(2), 6: lambda: spread_group(3)})
            pe.wait_ge(tb_lo, 4)
            open_pairs()
            transposes(1, 1)
            pe.wait_ge(bucketed_ready, 1)
            for t in range(1, first_sorted):
                if t + 1 < first_sorted:
                    transposes(t + 1, (t + 1) % RING)
                if t == 3:
                    pe.wait_ge(pairs_ready, NT)
                    open_pairs()
                if t >= 2:
                    scatter(t - 2, (t - 2) % RING)
                gather(t, t % RING)
            def last_scatters():
                for t in (first_sorted - 2, first_sorted - 1):
                    scatter(t, t % RING)

            products_of(HO_SRC, 0, {0: last_scatters},
                        {0: (logit_ready, first_sorted - 1), 2: (logit_ready, first_sorted)})
            pe.wait_ge(packed_ready, 1)
            product(HN_H, [(4, packed_rows(0))], True, True, open_after={4: (pairs_ready, 2 * NT)})
            products_of(HO_DST, 0, open_after={0: (tb_biased, 2 * NT)}, apart=SPLIT)
            pe.wait_ge(first_kept, 2)
            open_pairs()
            pe.wait_ge(route_ready, 1)

            def load(t, n):
                vals = nc.values_load_multi_w_load_instructions(
                    route[0:1, bass.ds(t - first_sorted, n), :].rearrange("p n i -> p (n i)"),
                    engines=[mybir.EngineType.PE], min_val=0, max_val=2 * NW * D,
                    skip_runtime_bounds_check_because="the sort clamps them")[1]
                limits = [(0, (NW - 1) * D), (NW * D, (2 * NW - 1) * D), (4 * BANK, 4 * BANK + (NB - 1) * WIN)]
                return [[nc.s_assert_within(vals[3 * j + i], *limits[i],
                                            skip_runtime_bounds_check_because="the sort clamps them") for i in range(3)]
                        for j in range(n)]

            def sorted_transposes(t, q):
                b = q % 2
                if q % 2 == 0:
                    ready = t + (2 - first_sorted)
                    pe.wait_ge(shot_ready, min(ready, ST) if isinstance(t, int) else ready)
                for j, part in enumerate((DST, SRC)):
                    twice = sorted_hot[:, q, part:part + 2, :].rearrange("p i n -> p (i n)")
                    ins = nc.tensor.transpose(p_tr[b][:, j * P:(j + 1) * P].bitcast(F32R), twice, ident_r[:, :])
                ins.then_inc(tr_done, 1)

            def sorted_gather(t, q, src_rows, dst_rows, _):
                b = q % 2
                pe.wait_ge(hotT_ready, t + 1)
                pe.wait_ge(logit_ready, t - 1)
                for j, at in enumerate((dst_rows, src_rows)):
                    for h in range(HALVES):
                        ins = nc.tensor.matmul(pz[b][:, h * BANK:(h + 1) * BANK], hotT[:, b, j, :],
                                               win_rows[:, h * BANK:][:, bass.ds(at, BANK)], start=(j == 0), stop=(j == 1))
                ins.then_inc(gather_done, 1)

            def sorted_scatter(t, q, _, __, at):
                pe.wait_ge(scaled_ready, t + 1)
                sums = psum[:, :, :].rearrange("p b n -> p (b n)")[:, bass.ds(at, WIN)]
                nc.tensor.matmul(sums, added[:, q, :, :].rearrange("p i n -> p (i n)"),
                                 sorted_hot[:, q, SRC, :].bitcast(F32),
                                 start=False, stop=False, skip_group_check=True).then_inc(scatter_done, 1)

            def sorted_round(first, q0, n, lead):
                routes = load(first - lead, min(4, lead + n))
                for j in range(n):
                    t, q = first + j, (q0 + j) % SORTED_RING
                    sorted_transposes(t + 1, (q + 1) % SORTED_RING)
                    sorted_gather(t, q, *routes[lead + j])
                    if len(routes) == lead + j + 1 < lead + n:
                        routes += load(t + 1, min(4, n - 1 - j))
                    if lead:
                        sorted_scatter(t - lead, (q - lead) % SORTED_RING, *routes[j])

            f, last, lead = first_sorted, all_tiles - 1, 2
            sorted_transposes(f, f % SORTED_RING)
            pe.wait_ge(tb_lo, 12)
            sorted_round(f, f % SORTED_RING, lead, 0)
            rounds, rest = divmod(ST - 1 - lead, SORTED_RING)
            with pe.Fori(0, rounds) as r:
                sorted_round(r * SORTED_RING + (f + lead), (f + lead) % SORTED_RING, SORTED_RING, lead)
            if rest:
                sorted_round(last - rest, (last - rest) % SORTED_RING, rest, lead)
            routes = load(last - lead, lead + 1)
            sorted_gather(last, last % SORTED_RING, *routes[lead])
            for j in range(lead + 1):
                t = last - lead + j
                sorted_scatter(t, t % SORTED_RING, *routes[j])

            pe.wait_ge(logit_ready, all_tiles)
            product(ON_H, [(6, h_rows(1)), (4, packed_rows(1))], True, False, open_after={4: (blocks_ready, 1)})
            pe.wait_ge(alpha_ready, NT)
            for s_tile in range(NT):
                for c in range(NT):
                    ins = nc.tensor.transpose(psum[:, 0, s_tile * N + c * P:s_tile * N + (c + 1) * P],
                                              alpha[:, c, s_tile * P:(s_tile + 1) * P], ident[:, :])
            ins.then_inc(alphaT_done, 1)
            pe.wait_ge(alphaT_ready, 1)

            def z_of(b):
                if b >= 2:
                    pe.wait_ge(z_lo, b - 1)
                for k in range(2 * b, 2 * b + 2):
                    for s_tile in range(NT):
                        ins = nc.tensor.matmul(psum[:, b % 2, (k % 2) * N:(k % 2 + 1) * N],
                                               h_sb[:, s_tile, k * P:(k + 1) * P], alphaT[:, s_tile, :],
                                               start=(s_tile == 0), stop=(s_tile == NT - 1))
                ins.then_inc(z_done, 1)

            def z_split(b):
                pe.wait_ge(z_lo, b + 1)
            z_of(0)
            z_of(1)
            z_split(0)
            z1_rows = split_rows(lambda c: z1[:, c, 0, :], lambda c: z1[:, c, 1, :])
            product(ON_Z, [(4, packed_rows(1)), (6, z1_rows)], False, True,
                    {0: lambda: z_of(2), 1: lambda: z_split(1), 2: lambda: z_of(3), 3: lambda: z_split(2),
                     5: lambda: z_split(3)})
            product(HN_Z, [(2, packed_rows(0), [h]) for h in range(HALVES)], True, True, apart=KC // 2)


_INS = ["x", "src", "dst", "L0_gnn_W_hh", "L0_gnn_b_hh", "L0_gnn_W_oo", "L0_gnn_b_oo", "L0_gnn_W_ho", "L0_gnn_b_ho",
        "L0_gnn_W_a", "L0_gnn_b_a", "L0_gnn_W_hn", "L0_gnn_b_hn", "L0_gnn_W_on", "L0_gnn_b_on"]


def kernel(**inputs):
    import numpy as _np
    import concourse.bacc as _bacc
    from concourse import mybir as _mybir
    from concourse.bass_utils import run_bass_kernel_spmd as _run

    nc = _bacc.Bacc("TRN2", target_bir_lowering=False, num_devices=1)
    arrays, ap = {}, {}
    for name in _INS:
        a = _np.ascontiguousarray(inputs[name])
        arrays[f"in_{name}"] = a
        ap[name] = nc.dram_tensor(f"in_{name}", a.shape, _mybir.dt.from_np(a.dtype), kind="ExternalInput").ap()
    shape = tuple(inputs["x"].shape)
    out = nc.dram_tensor("out_0", shape, _mybir.dt.float32, kind="ExternalOutput").ap()
    e_hh, e_oo = 128, 640
    w = lambda n: ap[f"L0_gnn_{n}"]
    gnn_kernel(nc, ap["x"], ap["src"], ap["dst"], [w("W_hh"), w("W_oo"), w("W_ho")], [w("b_hh"), w("b_oo"), w("b_ho")],
               w("W_a"), w("b_a"), [w("W_hn"), w("W_on")], [w("b_hn"), w("b_on")], out,
               [e_hh, e_oo, inputs["src"].shape[0] - e_hh - e_oo], 64)
    r = _run(nc, [arrays], core_ids=[0])
    return r.results[0]["out_0"]
```
